# Optimizing a Trainium2 kernel written in Bass

```python
import numpy as np
import jax
import jax.numpy as jnp

def _softmax(x, axis=-1):
    return jax.nn.softmax(x, axis=axis)

def _gelu(x):
    return jax.nn.gelu(x, approximate=True)

def _silu(x):
    return jax.nn.silu(x)

def _sigmoid(x):
    return jax.nn.sigmoid(x)

def _layernorm(x, axis=-1, eps=1e-05):
    m = jnp.mean(x, axis=axis, keepdims=True)
    v = jnp.var(x, axis=axis, keepdims=True)
    return (x - m) / jnp.sqrt(v + eps)

def _scatter_add(tgt, idx, src, axis=0):
    return tgt.at[idx].add(src)

def _segment_sum(src, seg, n):
    return jax.ops.segment_sum(src, seg, n)
kernel_name = 'mk_gnn_preln_d4_gnn_r16_68679e'

def setup_inputs(seed: int=0):
    np.random.seed(seed)
    _w = jnp.asarray

    def _rec_inputs():
        import jax
        import jax.numpy as jnp
        _gk = jax.random.key(seed)
        x = -0.000202 + 1 * jax.random.normal(jax.random.fold_in(_gk, 1), (3125, 128), jnp.float32)
        src = jax.random.randint(jax.random.fold_in(_gk, 2), (50000,), 0, 3125, jnp.int32)
        dst = jax.random.randint(jax.random.fold_in(_gk, 3), (50000,), 0, 3125, jnp.int32)
        _o = jnp.argsort(dst, stable=True)
        src = src[_o]
        dst = dst[_o]
        edge_attr_3 = -0.000201632 + 0.999762 * jax.random.normal(jax.random.fold_in(_gk, 12), (50000, 3), jnp.float32)
        edge_type_8 = jax.random.randint(jax.random.fold_in(_gk, 14), (50000,), 0, 8, jnp.int32)
        edge_weight = jax.random.uniform(jax.random.fold_in(_gk, 15), (50000,), jnp.float32, 0.0, 0.999998)
        return (x, src, dst, edge_attr_3, edge_type_8, edge_weight)
    x, src, dst, edge_attr_3, edge_type_8, edge_weight = _rec_inputs()

    def _L0_gnn_setup():
        import jax, jax.numpy as jnp
        import numpy as np
        N_NODES = 3125
        N_EDGES = 37500
        D = 128
        APPNP_K = 5
        APPNP_ALPHA = 0.2

        def _mish(x):
            return x * jnp.tanh(jax.nn.softplus(x))

        def _appnp(x0, src, dst):
            ones = jnp.ones((src.shape[0],), dtype=x0.dtype)
            deg_out = jnp.clip(jax.ops.segment_sum(ones, src, num_segments=N_NODES), 1.0)
            deg_in = jnp.clip(jax.ops.segment_sum(ones, dst, num_segments=N_NODES), 1.0)
            norm_o = deg_out[:, None] ** (-0.5)
            norm_i = deg_in[:, None] ** (-0.5)
            h = x0
            for _ in range(APPNP_K):
                h = h * norm_o
                h = jax.ops.segment_sum(h[src], dst, num_segments=N_NODES)
                h = h * norm_i
                h = (1.0 - APPNP_ALPHA) * h + APPNP_ALPHA * x0
            return h

        def _gin(h, src, dst, eps, W, b):
            agg = jax.ops.segment_sum(h[src], dst, num_segments=N_NODES)
            return ((1.0 + eps) * h + agg) @ W + b
        key = jax.random.key(seed)
        ks = jax.random.split(key, 6)
        x = jax.random.normal(ks[0], (N_NODES, D), dtype=jnp.float32)
        src = jax.random.randint(ks[1], (N_EDGES,), 0, N_NODES, dtype=jnp.int32)
        dst = jax.random.randint(ks[2], (N_EDGES,), 0, N_NODES, dtype=jnp.int32)
        W1 = jax.random.normal(ks[3], (D, D), dtype=jnp.float32) * (1.0 / np.sqrt(D))
        b1 = jnp.zeros((D,), dtype=jnp.float32)
        W2 = jax.random.normal(ks[4], (2 * D, D), dtype=jnp.float32) * (1.0 / np.sqrt(2 * D))
        b2 = jnp.zeros((D,), dtype=jnp.float32)
        eps1 = jnp.zeros((1,), dtype=jnp.float32)
        eps2 = jnp.zeros((1,), dtype=jnp.float32)
        return {'x': x, 'src': src, 'dst': dst, 'W1': W1, 'b1': b1, 'W2': W2, 'b2': b2, 'eps1': eps1, 'eps2': eps2}
    _L0_gnn_all = _L0_gnn_setup()
    _L0_gnn_in = {k: v for k, v in _L0_gnn_all.items() if k in ('W1', 'b1', 'W2', 'b2', 'eps1', 'eps2')}
    del _L0_gnn_all

    def _L1_gnn_setup():
        import jax, jax.numpy as jnp
        import numpy as np
        N_NODES = 3125
        N_EDGES = 32000
        HID = 128
        EDGE_DIM = 3
        N_LAYERS = 2
        LN_EPS = 1e-05

        def _mlp(h, W1, b1, W2, b2, g, beta):
            h = jax.nn.silu(h @ W1 + b1)
            h = jax.nn.silu(h @ W2 + b2)
            mu = jnp.mean(h, axis=-1, keepdims=True)
            var = jnp.mean(jnp.square(h - mu), axis=-1, keepdims=True)
            return g * (h - mu) * jax.lax.rsqrt(var + LN_EPS) + beta

        def _forward(x, edge_attr, emb_W1, emb_b1, emb_W2, emb_b2, emb_g, emb_beta, eW1, eb1, eW2, eb2, eg, ebeta, nW1, nb1, nW2, nb2, ng, nbeta, edge_index):
            src = edge_index[0]
            dst = edge_index[1]
            edge_attr = _mlp(edge_attr, emb_W1, emb_b1, emb_W2, emb_b2, emb_g, emb_beta)
            for l in range(N_LAYERS):
                x_i = x[dst]
                x_j = x[src]
                msg_in = jnp.concatenate([x_i, x_j, edge_attr], axis=1)
                edges_new = _mlp(msg_in, eW1[l], eb1[l], eW2[l], eb2[l], eg[l], ebeta[l]) + edge_attr
                agg = jax.ops.segment_sum(edges_new, dst, num_segments=N_NODES)
                node_in = jnp.concatenate([x, agg], axis=1)
                x = _mlp(node_in, nW1[l], nb1[l], nW2[l], nb2[l], ng[l], nbeta[l]) + x
                edge_attr = edges_new
            return x
        key = jax.random.key(seed)
        ks = jax.random.split(key, 10)
        s = 0.02
        L, H = (N_LAYERS, HID)
        return {'x': jax.random.normal(ks[0], (N_NODES, H), dtype=jnp.float32), 'edge_attr': jax.random.normal(ks[1], (N_EDGES, EDGE_DIM), dtype=jnp.float32), 'emb_W1': jax.random.normal(ks[2], (EDGE_DIM, H), dtype=jnp.float32) * s, 'emb_b1': jnp.zeros((H,), jnp.float32), 'emb_W2': jax.random.normal(ks[3], (H, H), dtype=jnp.float32) * s, 'emb_b2': jnp.zeros((H,), jnp.float32), 'emb_g': jnp.ones((H,), jnp.float32), 'emb_beta': jnp.zeros((H,), jnp.float32), 'eW1': jax.random.normal(ks[4], (L, 3 * H, H), dtype=jnp.float32) * s, 'eb1': jnp.zeros((L, H), jnp.float32), 'eW2': jax.random.normal(ks[5], (L, H, H), dtype=jnp.float32) * s, 'eb2': jnp.zeros((L, H), jnp.float32), 'eg': jnp.ones((L, H), jnp.float32), 'ebeta': jnp.zeros((L, H), jnp.float32), 'nW1': jax.random.normal(ks[6], (L, 2 * H, H), dtype=jnp.float32) * s, 'nb1': jnp.zeros((L, H), jnp.float32), 'nW2': jax.random.normal(ks[7], (L, H, H), dtype=jnp.float32) * s, 'nb2': jnp.zeros((L, H), jnp.float32), 'ng': jnp.ones((L, H), jnp.float32), 'nbeta': jnp.zeros((L, H), jnp.float32), 'edge_index': jax.random.randint(ks[8], (2, N_EDGES), 0, N_NODES, dtype=jnp.int32).astype(jnp.int64)}
    _L1_gnn_all = _L1_gnn_setup()
    _L1_gnn_in = {k: v for k, v in _L1_gnn_all.items() if k in ('emb_W1', 'emb_b1', 'emb_W2', 'emb_b2', 'emb_g', 'emb_beta', 'eW1', 'eb1', 'eW2', 'eb2', 'eg', 'ebeta', 'nW1', 'nb1', 'nW2', 'nb2', 'ng', 'nbeta')}
    del _L1_gnn_all

    def _L2_gnn_setup():
        import jax, jax.numpy as jnp
        import numpy as np
        N = 3125
        E = 50000
        IN_F = 128
        OUT_F = 128
        key = jax.random.key(seed)
        k1, k2, k3, k4, k5 = jax.random.split(key, 5)
        x = jax.random.normal(k1, (N, IN_F), dtype=jnp.float32)
        edge_index = jax.random.randint(k2, (2, E), 0, N, dtype=jnp.int64)
        edge_weight = jax.random.uniform(k3, (E,), dtype=jnp.float32)
        W = jax.random.normal(k4, (OUT_F, IN_F), dtype=jnp.float32) * (1.0 / np.sqrt(IN_F))
        b = jax.random.normal(k5, (OUT_F,), dtype=jnp.float32) * 0.01
        return {'x': x, 'edge_index': edge_index, 'edge_weight': edge_weight, 'W': W, 'b': b}
    _L2_gnn_all = _L2_gnn_setup()
    _L2_gnn_in = {k: v for k, v in _L2_gnn_all.items() if k in ('W', 'b')}
    del _L2_gnn_all

    def _L3_gnn_setup():
        import jax, jax.numpy as jnp
        import numpy as np
        NUM_HEADS = 8
        NEG_SLOPE = 0.2

        def typed_linear(x, W, etype):
            out = jnp.zeros((x.shape[0], W.shape[2]), x.dtype)
            for t in range(W.shape[0]):
                out = out + jnp.where((etype == t)[:, None], x @ W[t], jnp.zeros((), x.dtype))
            return out
        key = jax.random.key(seed)
        ks = jax.random.split(key, 9)
        N, E, IN = (3125, 50000, 128)
        H, D = (NUM_HEADS, 16)
        HD = H * D
        T = 8
        s = 0.05
        return {'x': jax.random.normal(ks[0], (N, IN), jnp.float32), 'src': jax.random.randint(ks[1], (E,), 0, N), 'dst': jax.random.randint(ks[2], (E,), 0, N), 'etype': jax.random.randint(ks[3], (E,), 0, T), 'W_w': jax.random.normal(ks[4], (T, IN, HD), jnp.float32) * s, 'W_al': jax.random.normal(ks[5], (T, HD, HD), jnp.float32) * s, 'W_ar': jax.random.normal(ks[6], (T, HD, HD), jnp.float32) * s, 'W_res': jax.random.normal(ks[7], (IN, HD), jnp.float32) * s, 'b_res': jnp.zeros((HD,), jnp.float32)}
    _L3_gnn_all = _L3_gnn_setup()
    _L3_gnn_in = {k: v for k, v in _L3_gnn_all.items() if k in ('W_w', 'W_al', 'W_ar', 'W_res', 'b_res')}
    del _L3_gnn_all
    return {'x': x, 'src': src, 'dst': dst, 'edge_attr_3': edge_attr_3, 'edge_type_8': edge_type_8, 'edge_weight': edge_weight, 'L0_gnn_W1': _L0_gnn_in['W1'], 'L0_gnn_b1': _L0_gnn_in['b1'], 'L0_gnn_W2': _L0_gnn_in['W2'], 'L0_gnn_b2': _L0_gnn_in['b2'], 'L0_gnn_eps1': _L0_gnn_in['eps1'], 'L0_gnn_eps2': _L0_gnn_in['eps2'], 'L1_gnn_emb_W1': _L1_gnn_in['emb_W1'], 'L1_gnn_emb_b1': _L1_gnn_in['emb_b1'], 'L1_gnn_emb_W2': _L1_gnn_in['emb_W2'], 'L1_gnn_emb_b2': _L1_gnn_in['emb_b2'], 'L1_gnn_emb_g': _L1_gnn_in['emb_g'], 'L1_gnn_emb_beta': _L1_gnn_in['emb_beta'], 'L1_gnn_eW1': _L1_gnn_in['eW1'], 'L1_gnn_eb1': _L1_gnn_in['eb1'], 'L1_gnn_eW2': _L1_gnn_in['eW2'], 'L1_gnn_eb2': _L1_gnn_in['eb2'], 'L1_gnn_eg': _L1_gnn_in['eg'], 'L1_gnn_ebeta': _L1_gnn_in['ebeta'], 'L1_gnn_nW1': _L1_gnn_in['nW1'], 'L1_gnn_nb1': _L1_gnn_in['nb1'], 'L1_gnn_nW2': _L1_gnn_in['nW2'], 'L1_gnn_nb2': _L1_gnn_in['nb2'], 'L1_gnn_ng': _L1_gnn_in['ng'], 'L1_gnn_nbeta': _L1_gnn_in['nbeta'], 'L2_gnn_W': _L2_gnn_in['W'], 'L2_gnn_b': _L2_gnn_in['b'], 'L3_gnn_W_w': _L3_gnn_in['W_w'], 'L3_gnn_W_al': _L3_gnn_in['W_al'], 'L3_gnn_W_ar': _L3_gnn_in['W_ar'], 'L3_gnn_W_res': _L3_gnn_in['W_res'], 'L3_gnn_b_res': _L3_gnn_in['b_res']}

def reference(x, src, dst, edge_attr_3, edge_type_8, edge_weight, L0_gnn_W1, L0_gnn_b1, L0_gnn_W2, L0_gnn_b2, L0_gnn_eps1, L0_gnn_eps2, L1_gnn_emb_W1, L1_gnn_emb_b1, L1_gnn_emb_W2, L1_gnn_emb_b2, L1_gnn_emb_g, L1_gnn_emb_beta, L1_gnn_eW1, L1_gnn_eb1, L1_gnn_eW2, L1_gnn_eb2, L1_gnn_eg, L1_gnn_ebeta, L1_gnn_nW1, L1_gnn_nb1, L1_gnn_nW2, L1_gnn_nb2, L1_gnn_ng, L1_gnn_nbeta, L2_gnn_W, L2_gnn_b, L3_gnn_W_w, L3_gnn_W_al, L3_gnn_W_ar, L3_gnn_W_res, L3_gnn_b_res):
    import jax
    import jax.numpy as jnp

    def _L0_gnn_ref(x, src, dst, W1, b1, W2, b2, eps1, eps2):
        import jax, jax.numpy as jnp
        import numpy as np
        N_NODES = 3125
        N_EDGES = 37500
        D = 128
        APPNP_K = 5
        APPNP_ALPHA = 0.2

        def _mish(x):
            return x * jnp.tanh(jax.nn.softplus(x))

        def _appnp(x0, src, dst):
            ones = jnp.ones((src.shape[0],), dtype=x0.dtype)
            deg_out = jnp.clip(jax.ops.segment_sum(ones, src, num_segments=N_NODES), 1.0)
            deg_in = jnp.clip(jax.ops.segment_sum(ones, dst, num_segments=N_NODES), 1.0)
            norm_o = deg_out[:, None] ** (-0.5)
            norm_i = deg_in[:, None] ** (-0.5)
            h = x0
            for _ in range(APPNP_K):
                h = h * norm_o
                h = jax.ops.segment_sum(h[src], dst, num_segments=N_NODES)
                h = h * norm_i
                h = (1.0 - APPNP_ALPHA) * h + APPNP_ALPHA * x0
            return h

        def _gin(h, src, dst, eps, W, b):
            agg = jax.ops.segment_sum(h[src], dst, num_segments=N_NODES)
            return ((1.0 + eps) * h + agg) @ W + b
        out = jnp.tanh(x)
        x0 = out
        out = _appnp(out, src, dst)
        out = _gin(out, src, dst, eps1[0], W1, b1)
        out = jnp.concatenate([out, x0], axis=1)
        out = _gin(out, src, dst, eps2[0], W2, b2)
        return _mish(out)

    def _L1_gnn_ref(x, edge_attr, emb_W1, emb_b1, emb_W2, emb_b2, emb_g, emb_beta, eW1, eb1, eW2, eb2, eg, ebeta, nW1, nb1, nW2, nb2, ng, nbeta, edge_index):
        import jax, jax.numpy as jnp
        import numpy as np
        N_NODES = 3125
        N_EDGES = 32000
        HID = 128
        EDGE_DIM = 3
        N_LAYERS = 2
        LN_EPS = 1e-05

        def _mlp(h, W1, b1, W2, b2, g, beta):
            h = jax.nn.silu(h @ W1 + b1)
            h = jax.nn.silu(h @ W2 + b2)
            mu = jnp.mean(h, axis=-1, keepdims=True)
            var = jnp.mean(jnp.square(h - mu), axis=-1, keepdims=True)
            return g * (h - mu) * jax.lax.rsqrt(var + LN_EPS) + beta

        def _forward(x, edge_attr, emb_W1, emb_b1, emb_W2, emb_b2, emb_g, emb_beta, eW1, eb1, eW2, eb2, eg, ebeta, nW1, nb1, nW2, nb2, ng, nbeta, edge_index):
            src = edge_index[0]
            dst = edge_index[1]
            edge_attr = _mlp(edge_attr, emb_W1, emb_b1, emb_W2, emb_b2, emb_g, emb_beta)
            for l in range(N_LAYERS):
                x_i = x[dst]
                x_j = x[src]
                msg_in = jnp.concatenate([x_i, x_j, edge_attr], axis=1)
                edges_new = _mlp(msg_in, eW1[l], eb1[l], eW2[l], eb2[l], eg[l], ebeta[l]) + edge_attr
                agg = jax.ops.segment_sum(edges_new, dst, num_segments=N_NODES)
                node_in = jnp.concatenate([x, agg], axis=1)
                x = _mlp(node_in, nW1[l], nb1[l], nW2[l], nb2[l], ng[l], nbeta[l]) + x
                edge_attr = edges_new
            return x
        return _forward(x, edge_attr, emb_W1, emb_b1, emb_W2, emb_b2, emb_g, emb_beta, eW1, eb1, eW2, eb2, eg, ebeta, nW1, nb1, nW2, nb2, ng, nbeta, edge_index)

    def _L2_gnn_ref(x, edge_index, edge_weight, W, b):
        import jax, jax.numpy as jnp
        import numpy as np
        N = 3125
        E = 50000
        IN_F = 128
        OUT_F = 128
        hidden = jnp.einsum('ni,oi->no', x, W) + b
        dst = edge_index[0]
        src = edge_index[1]
        msgs = edge_weight[:, None] * hidden[src]
        out = jax.ops.segment_sum(msgs, dst, num_segments=x.shape[0])
        return out

    def _L3_gnn_ref(x, src, dst, etype, W_w, W_al, W_ar, W_res, b_res):
        import jax, jax.numpy as jnp
        import numpy as np
        NUM_HEADS = 8
        NEG_SLOPE = 0.2

        def typed_linear(x, W, etype):
            out = jnp.zeros((x.shape[0], W.shape[2]), x.dtype)
            for t in range(W.shape[0]):
                out = out + jnp.where((etype == t)[:, None], x @ W[t], jnp.zeros((), x.dtype))
            return out
        N = x.shape[0]
        HD = W_w.shape[2]
        H = NUM_HEADS
        D = HD // H
        m = x[src]
        feat = typed_linear(m, W_w, etype)
        h = feat
        h_l = typed_linear(h, W_al, etype).reshape(-1, H, D).sum(-1)
        h_r = typed_linear(h, W_ar, etype).reshape(-1, H, D).sum(-1)
        att = jax.nn.leaky_relu(h_l + h_r, NEG_SLOPE)
        att_max = jax.ops.segment_max(att, dst, num_segments=N)
        att_exp = jnp.exp(att - att_max[dst])
        denom = jax.ops.segment_sum(att_exp, dst, num_segments=N)
        att = att_exp / denom[dst]
        alpha = jnp.einsum('ehd,eh->ed', h.reshape(-1, H, D), att)
        del alpha
        emb = jax.ops.segment_sum(h, dst, num_segments=N)
        out = emb + x @ W_res + b_res
        return jax.nn.elu(out)
    edge_index = jnp.stack([src, dst])
    h = jnp.maximum(_layernorm(x, axis=-1), 0.0)
    x = x + _L0_gnn_ref(h, src, dst, L0_gnn_W1, L0_gnn_b1, L0_gnn_W2, L0_gnn_b2, L0_gnn_eps1, L0_gnn_eps2)
    h = jnp.maximum(_layernorm(x, axis=-1), 0.0)
    x = x + _L1_gnn_ref(h, edge_attr_3, L1_gnn_emb_W1, L1_gnn_emb_b1, L1_gnn_emb_W2, L1_gnn_emb_b2, L1_gnn_emb_g, L1_gnn_emb_beta, L1_gnn_eW1, L1_gnn_eb1, L1_gnn_eW2, L1_gnn_eb2, L1_gnn_eg, L1_gnn_ebeta, L1_gnn_nW1, L1_gnn_nb1, L1_gnn_nW2, L1_gnn_nb2, L1_gnn_ng, L1_gnn_nbeta, edge_index)
    h = jnp.maximum(_layernorm(x, axis=-1), 0.0)
    x = x + _L2_gnn_ref(h, edge_index, edge_weight, L2_gnn_W, L2_gnn_b)
    h = jnp.maximum(_layernorm(x, axis=-1), 0.0)
    x = x + _L3_gnn_ref(h, src, dst, edge_type_8, L3_gnn_W_w, L3_gnn_W_al, L3_gnn_W_ar, L3_gnn_W_res, L3_gnn_b_res)
    return x

_drawn_inputs = setup_inputs


def setup_inputs(seed=0):
    import zlib

    import numpy as np

    out = dict(_drawn_inputs(seed))
    spreads = {'L0_gnn_b1': (0.0, 0.418),
     'L0_gnn_b2': (0.0, 2.0),
     'L1_gnn_emb_b1': (0.0, 2.0),
     'L1_gnn_emb_b2': (0.0, 2.0),
     'L1_gnn_emb_g': (1.0, 0.6),
     'L1_gnn_emb_beta': (0.0, 2.0),
     'L1_gnn_eb1': (0.0, 2.0),
     'L1_gnn_eb2': (0.0, 2.0),
     'L1_gnn_eg': (1.0, 0.6),
     'L1_gnn_ebeta': (0.0, 2.0),
     'L1_gnn_nb1': (0.0, 2.0),
     'L1_gnn_nb2': (0.0, 0.8),
     'L1_gnn_ng': (1.0, 0.6),
     'L1_gnn_nbeta': (0.0, 2.0),
     'L3_gnn_b_res': (0.0, 2.0)}
    factors = {'edge_attr_3': 64.0,
     'edge_weight': 3.13,
     'L1_gnn_emb_W1': 46.083,
     'L1_gnn_emb_W2': 25.539,
     'L1_gnn_eW1': 17.331,
     'L1_gnn_eW2': 4.549,
     'L2_gnn_b': 8.0,
     'L3_gnn_W_res': 6.957}
    for name, (base, spread) in spreads.items():
        noise = np.random.default_rng([zlib.crc32(name.encode()), seed]).standard_normal(out[name].shape)
        drawn = base * np.exp(spread * noise) if base else spread * noise
        out[name] = jnp.asarray(drawn.astype(out[name].dtype))
    for name, factor in factors.items():
        out[name] = (out[name] * factor).astype(out[name].dtype)
    return out
```

```python
import concourse.bass as bass
from concourse import mybir
from contextlib import ExitStack

F32 = mybir.dt.float32
I32 = mybir.dt.int32
BF16 = mybir.dt.bfloat16
FP16 = mybir.dt.float16
ALU = mybir.AluOpType
ACT = mybir.ActivationFunctionType
AX = mybir.AxisListType.X

P = 128
D = 128
N = 3125
E = 50000
NT = (N + P - 1) // P
NLAST = N - (NT - 1) * P
NB = (NT + 3) // 4
NW = NB * 4
EP, EC = 125, 400
GS = 512
G = (E + NT * (GS - 1)) // GS
SLOTS = G * GS
US = 256
GU = -(-((E + NT * (US - 1)) // US) // (GS // US))
REC = 8
REC2 = 4
REC_ROWS = E + GS
LN_EPS = 1e-5
ALPHA = 0.2
HOPS = 5


class Phase:

    def __init__(self, nc, name):
        self.nc, self.name, self.stack, self.sems = nc, name, ExitStack(), []

    def sb(self, name, shape, dt=F32):
        return self.stack.enter_context(self.nc.sbuf_tensor(f"{self.name}_{name}", shape, dt))

    def ps(self, name, shape, dt=F32):
        return self.stack.enter_context(self.nc.psum_tensor(f"{self.name}_{name}", shape, dt))

    def sem(self, name):
        s = self.nc.alloc_semaphore(f"{self.name}_{name}")
        self.sems.append(s)
        return s

    def block(self):
        return self.nc.Block()

    def close(self):
        self.nc.clear_and_free_semaphores(self.sems)
        self.nc.all_engine_barrier()
        self.stack.close()


class Chain:

    def __init__(self, eng, sem, base=0):
        self.eng, self.sem, self.base, self.n = eng, sem, base, 0

    def __call__(self, ins):
        ins.then_inc(self.sem, 1)
        self.n += 1
        self.eng.wait_ge(self.sem, self.base + self.n)

    def turn(self, base):
        self.base, self.n = base, 0


def load_nodes(eng, tile, src, sem):
    half = NT // 2
    for a, b in ((0, half), (half, NT - 1)):
        eng.dma_start(tile[:, a:b, :],
                      src[a * P:b * P, :].rearrange("(t p) d -> p t d", p=P)).then_inc(sem, 16)
    eng.dma_start(tile[0:NLAST, NT - 1, :], src[(NT - 1) * P:N, :]).then_inc(sem, 16)


def constants(nc, K):
    ph = Phase(nc, "const")
    s_io, s_id, s_cp = ph.sem("iotas"), ph.sem("zeroed"), ph.sem("copied")
    with ph.block() as block:
        @block.gpsimd
        def _(pool):
            nc.gpsimd.iota(K.iota_row[:, :], pattern=[[1, GS]], base=0, channel_multiplier=0,
                           allow_small_or_imprecise_dtypes=True)
            nc.gpsimd.iota(K.iota_p[:, :], pattern=[[0, 1]], base=0, channel_multiplier=1,
                           allow_small_or_imprecise_dtypes=True).then_inc(s_io, 1)
            nc.gpsimd.memset(K.ident[:, :], 0.0).then_inc(s_id, 1)
            nc.gpsimd.memset(K.neghalf[:, :], -0.5)
            pool.wait_ge(s_id, 1)
            nc.gpsimd.affine_select(out=K.ident[:, :], in_=K.ident[:, :], compare_op=ALU.not_equal,
                                    fill=1.0, base=0, pattern=[[-1, P]], channel_multiplier=1)

        @block.vector
        def _(dve):
            nc.vector.memset(K.ones[:, :], 1.0)
            nc.vector.memset(K.ones_bf[:, :], 1.0)
            nc.vector.memset(K.deg[:, :, :], 0.0)
    ph.close()


def edge_layout(nc, A, K, lay, cuts):
    ph = Phase(nc, "lay" + str(lay.key))
    by_dst = lay.key == 1
    raw = ph.sb("raw", [EP, 3, EC], I32)
    wts = ph.sb("wts", [EP, EC])
    att = ph.sb("att", [EP, EC * 3])
    rec = ph.sb("rec", [EP, EC, lay.fields])
    tile_i = ph.sb("tile_i", [EP, EC], I32)
    tile_f = ph.sb("tile_f", [EP, EC])
    iota_t = ph.sb("iota_t", [P, NT])
    keep = ph.sb("keep", [EP, NT, EC], BF16)
    hot = ph.sb("hot", [EP, NT, EC], BF16)
    pre = ph.sb("pre", [EP, NT, EC])
    tri = ph.sb("tri", [EP, P])
    order = ph.sb("order", [EP, EC])
    rank = ph.sb("rank", [EP, EC])
    rank_i = ph.sb("rank_i", [EP, EC], I32)
    count = ph.sb("count", [EP, NT])
    excl = ph.sb("excl", [EP, NT])
    moved = ph.sb("moved", [EP, 1])
    moved_i = ph.sb("moved_i", [1, 1], I32)
    row = ph.sb("row", [P, 8, NT])
    row_i = ph.sb("row_i", [P, 2, NT], I32)
    grp = ph.sb("grp", [P, 8])
    row_zero = ph.sb("row_zero", [P, GS * lay.fields // P])
    side_idx = ph.sb("side_idx", [EP, 1], I32)
    side_rec = ph.sb("side_rec", [EP, REC])
    TOT, NGR, GEND, SEND, SBEG, SHIFT, MASK, PROD = range(8)
    GUNIT, GTILE, GBASE = range(3)
    p_small = ph.ps("p_small", [P, 512])
    p_flag = ph.ps("p_flag", [P, 512])
    tiles = [ph.sb(f"tiles{i}", [1, cut.per * P], I32) for i, cut in enumerate(cuts)]
    s_tiles, s_tilest = ph.sem("tiles"), ph.sem("tiles_stored")
    p_row = [ph.ps(f"p_row{i}", [P, 512]) for i in range(len(cuts))]
    s_ld, s_iota, s_cnt, s_sum, s_mv, s_mvs, s_flag, s_rec, s_z, s_zst, s_ch, s_pool, s_recst, s_side = (
        ph.sem(x) for x in ("loaded", "iotas", "counted", "summed", "moved", "moved_sum", "flag",
                            "records", "zeros", "zeros_stored", "chain", "pool_chain", "stored", "side"))
    s_tr, s_turn, s_ranked, s_cut = ph.sem("tiles_T"), ph.sem("turn"), ph.sem("ranked"), ph.sem("cut")

    with ph.block() as block:
        @block.sync
        def _(sp):
            for i, name in enumerate(("src", "dst", "edge_type_8")):
                sp.dma_start(raw[:, i, :], A[name].rearrange("(p c) -> p c", c=EC)).then_inc(s_ld, 16)
            sp.dma_start(wts[:, :], A["edge_weight"].rearrange("(p c) -> p c", c=EC)).then_inc(s_ld, 16)
            sp.dma_start(att[:, :], A["edge_attr_3"].rearrange("(p c) a -> p (c a)", c=EC)).then_inc(s_ld, 16)
            sp.wait_ge(s_z, 1)
            sp.dma_start(lay.rec[E:E + GS, :].rearrange("(p c) f -> p (c f)", p=P), row_zero[:, :])\
              .then_inc(s_zst, 16)
            sp.wait_ge(s_zst, 16)
            if not by_dst:
                sp.wait_ge(s_rec, 1)
                sp.dma_start(lay.unsorted[:, :], rec[:, :, :].rearrange("p c f -> p (c f)")).then_inc(s_recst, 16)
                sp.wait_ge(s_ranked, 1)
                sp.dma_start(lay.rank[:, :], rank_i[:, :]).then_inc(s_recst, 16)
                sp.wait_ge(s_recst, 32)
            for i, cut in enumerate(cuts):
                sp.wait_ge(s_tiles, i + 1)
                sp.dma_start(cut.tiles, tiles[i][:, :]).then_inc(s_tilest, 16)
            sp.wait_ge(s_tilest, 16 * len(cuts))

        @block.gpsimd
        def _(pool):
            nc.gpsimd.iota(iota_t[:, :], pattern=[[1, NT]], base=0, channel_multiplier=0,
                           allow_small_or_imprecise_dtypes=True)
            nc.gpsimd.iota(tri[:, :], pattern=[[1, P]], base=0, channel_multiplier=-1,
                           allow_small_or_imprecise_dtypes=True)
            nc.gpsimd.iota(order[:, :], pattern=[[1, EC]], base=0, channel_multiplier=EC,
                           allow_small_or_imprecise_dtypes=True).then_inc(s_iota, 1)
            pool.wait_ge(s_rec, 1)
            pool.wait_ge(s_flag, 1)
            if not by_dst:
                return
            flag = pool.value_load(moved_i[0:1, 0:1], min_val=0, max_val=E)
            with pool.If(flag == 0):
                pool.dma_start(lay.rec[0:E, :].rearrange("(p c) f -> p (c f)", c=EC),
                               rec[:, :, :].rearrange("p c f -> p (c f)")).then_inc(s_recst, 16)
                pool.wait_ge(s_recst, 16)
            with pool.Else():
                with pool.Fori(0, EC) as c:
                    nc.gpsimd.tensor_copy(side_idx[:, :], rank_i[:, bass.ds(c, 1)])
                    nc.gpsimd.tensor_copy(side_rec[:, :], rec[:, bass.ds(c, 1), :]).then_inc(s_pool, 1)
                    pool.wait_ge(s_pool, c + 1)
                    pool.sem_inc(s_turn, 1)
                    pool.indirect_dma_start(
                        out=lay.rec[:, :], out_offset=bass.IndirectOffsetOnAxis(ap=side_idx[:, 0:1], axis=0),
                        in_=side_rec[:, :], in_offset=None).then_inc(s_side, 16)
                    pool.wait_ge(s_side, (c + 1) * 16)

        @block.tensor
        def _(pe):
            pe.wait_ge(s_cnt, 1)
            nc.tensor.matmul(p_small[:, 0:NT], tri[:, :], count[:, :], start=True, stop=True)
            nc.tensor.matmul(p_small[:, NT:2 * NT], K.ones[0:EP, :], count[:, :], start=True, stop=True)\
              .then_inc(s_sum, 1)
            pe.wait_ge(s_mv, 1)
            nc.tensor.matmul(p_flag[:, 0:1], K.ones[0:EP, :], moved[:, :], start=True, stop=True)\
              .then_inc(s_mvs, 1)
            pe.wait_ge(s_cut, sum(cut.per for cut in cuts))
            for i, cut in enumerate(cuts):
                for k in range(cut.per):
                    ins = nc.tensor.matmul(p_row[i][0:1, k * P:(k + 1) * P], cut.grp[:, 2, k:k + 1], K.ident[:, :],
                                           start=True, stop=True)
            ins.then_inc(s_tr, 1)

        @block.vector
        def _(dve):
            ch = Chain(dve, s_ch)
            nc.vector.memset(row_zero[:, :], 0.0).then_inc(s_z, 1)
            nc.vector.memset(rec[:, :, lay.fields - 1:lay.fields], 0.0)
            ch(nc.vector.memset(keep[:, :, :], 1.0))
            ch(nc.vector.memset(keep[:, :, 0:1], 0.0))
            dve.wait_ge(s_iota, 1)
            ch(nc.vector.tensor_scalar(tri[:, :], tri[:, :], 0.5, None, ALU.is_gt))
            dve.wait_ge(s_ld, 80)
            f = lambda i: rec[:, :, i:i + 1].rearrange("p c f -> p (c f)")
            if by_dst:
                for i in range(3):
                    nc.vector.tensor_copy(f(i), raw[:, i, :])
                nc.vector.tensor_copy(f(3), wts[:, :])
                nc.vector.tensor_copy(rec[:, :, 4:7], att[:, :].rearrange("p (c a) -> p c a", a=3)).then_inc(s_rec, 1)
            else:
                nc.vector.tensor_copy(f(0), raw[:, 1, :])
                nc.vector.tensor_copy(f(1), raw[:, 0, :])
                nc.vector.tensor_copy(f(2), wts[:, :]).then_inc(s_rec, 1)
            ch(nc.vector.tensor_scalar(tile_i[:, :], raw[:, lay.key, :], 7, None, ALU.arith_shift_right))
            ch(nc.vector.tensor_copy(tile_f[:, :], tile_i[:, :]))
            ch(nc.vector.tensor_tensor(hot[:, :, :], tile_f[:, :].unsqueeze(1).to_broadcast([EP, NT, EC]),
                                       iota_t[0:EP, :].unsqueeze(2).to_broadcast([EP, NT, EC]), ALU.is_equal))
            ch(nc.vector.tensor_tensor_scan(pre[:, :, :].rearrange("p t c -> p (t c)"),
                                            keep[:, :, :].rearrange("p t c -> p (t c)"),
                                            hot[:, :, :].rearrange("p t c -> p (t c)"),
                                            0.0, ALU.mult, ALU.add))
            nc.vector.tensor_copy(count[:, :], pre[:, :, EC - 1:EC].rearrange("p t c -> p (t c)")).then_inc(s_cnt, 1)
            dve.wait_ge(s_sum, 1)
            nc.vector.tensor_copy(excl[:, :], p_small[0:EP, 0:NT])
            ch(nc.vector.tensor_copy(row[:, TOT, :], p_small[:, NT:2 * NT]))
            ch(nc.vector.tensor_tensor_scan(row[:, SEND, :], K.ones[:, 0:NT], row[:, TOT, :], 0.0, ALU.mult, ALU.add))
            ch(nc.vector.tensor_tensor(row[:, SBEG, :], row[:, SEND, :], row[:, TOT, :], ALU.subtract))
            ch(nc.vector.scalar_tensor_tensor(excl[:, :], excl[:, :], -1.0, row[0:EP, SBEG, :], ALU.add, ALU.add))
            ch(nc.vector.tensor_tensor(pre[:, :, :], pre[:, :, :], excl[:, :].unsqueeze(2).to_broadcast([EP, NT, EC]),
                                       ALU.add))
            ch(nc.vector.tensor_tensor(pre[:, :, :], pre[:, :, :], hot[:, :, :], ALU.mult))
            ch(nc.vector.tensor_reduce(rank[:, :], pre[:, :, :].rearrange("p t c -> p c t"), AX, ALU.add))
            nc.vector.tensor_copy(rank_i[:, :], rank[:, :]).then_inc(s_ranked, 1)
            dve.wait_ge(s_ranked, 1)
            ch(nc.vector.tensor_tensor(rank[:, :], rank[:, :], order[:, :], ALU.not_equal))
            nc.vector.tensor_reduce(moved[:, :], rank[:, :], AX, ALU.add).then_inc(s_mv, 1)
            dve.wait_ge(s_mvs, 1)
            nc.vector.tensor_copy(moved_i[:, :], p_flag[0:1, 0:1]).then_inc(s_flag, 1)
            for cut in cuts:
                ch(nc.vector.tensor_scalar(row_i[:, 0, :], row[:, TOT, :], float(cut.unit - 1), None, ALU.add))
                ch(nc.vector.tensor_scalar(row_i[:, 1, :], row_i[:, 0, :], cut.unit.bit_length() - 1, None,
                                           ALU.arith_shift_right))
                ch(nc.vector.tensor_copy(row[:, NGR, :], row_i[:, 1, :]))
                ch(nc.vector.tensor_tensor_scan(row[:, GEND, :], K.ones[:, 0:NT], row[:, NGR, :], 0.0, ALU.mult, ALU.add))
                ch(nc.vector.tensor_tensor(row[:, SHIFT, :], row[:, GEND, :], row[:, NGR, :], ALU.subtract))
                ch(nc.vector.scalar_tensor_tensor(row[:, SHIFT, :], row[:, SHIFT, :], -float(cut.unit), row[:, SBEG, :],
                                                  ALU.mult, ALU.add))
                for k in range(cut.per):
                    unit, tile, base = (grp[:, i:i + 1] for i in (GUNIT, GTILE, GBASE))
                    off, end, at = (cut.grp[:, i, k:k + 1] for i in range(3))
                    ch(nc.vector.tensor_scalar(unit, K.iota_p[:, 0:1], float(cut.per), float(k), ALU.mult, ALU.add))
                    ch(nc.vector.tensor_scalar(row[:, MASK, :], row[:, GEND, :], unit, None, ALU.is_le))
                    ch(nc.vector.tensor_reduce(tile, row[:, MASK, :], AX, ALU.add))
                    ch(nc.vector.tensor_scalar(row[:, MASK, :], iota_t[:, :], tile, None, ALU.is_equal))
                    ch(nc.vector.tensor_tensor(row[:, PROD, :], row[:, MASK, :], row[:, SHIFT, :], ALU.mult))
                    ch(nc.vector.tensor_reduce(base, row[:, PROD, :], AX, ALU.add))
                    ch(nc.vector.tensor_tensor(row[:, PROD, :], row[:, MASK, :], row[:, SEND, :], ALU.mult))
                    ch(nc.vector.tensor_reduce(end, row[:, PROD, :], AX, ALU.add))
                    ch(nc.vector.scalar_tensor_tensor(off, unit, float(cut.unit), base, ALU.mult, ALU.add))
                    ch(nc.vector.tensor_scalar(off, off, float(E), None, ALU.min))
                    nc.vector.tensor_copy(cut.off_i[:, k:k + 1], off)
                    ch(nc.vector.tensor_scalar(tile, tile, float(NT - 1), None, ALU.min))
                    nc.vector.tensor_scalar(at, tile, float(P), None, ALU.mult).then_inc(s_cut, 1)
            dve.wait_ge(s_tr, 1)
            for i, cut in enumerate(cuts):
                nc.vector.tensor_copy(tiles[i][:, :].rearrange("a (g k) -> a k g", k=cut.per),
                                      p_row[i][0:1, 0:cut.per * P].rearrange("a (k g) -> a k g", k=cut.per))\
                    .then_inc(s_tiles, 1)
            if by_dst:
                nc.vector.tensor_copy(lay.tile_row[:, :], p_row[0][0:1, 0:P])
    ph.close()


def edge_tables(nc, K, dr, lay):
    ph = Phase(nc, "tab" + lay.name)
    by_dst = lay.key == 1
    typed = by_dst and lay.per > 1
    G, n_tab, S = lay.groups, lay.n_tab, lay.unit
    rec = ph.sb("rec", [G, GS, lay.fields])
    valid = ph.sb("valid", [G, GS])
    tab = ph.sb("tab", [G, n_tab, GS])
    tmp_i = ph.sb("tmp_i", [G, 2, GS], I32)
    att = ph.sb("att", [G, 3, GS])
    dl_bf = ph.sb("dl_bf", [G, GS], BF16)
    out = ph.sb("out", [P, n_tab, G * 4])
    SRC, IDX3, DL, W, SLOC, COMB = range(6)
    pieces = [(k, slice(k * S, (k + 1) * S)) for k in range(lay.per)]
    p_t = [ph.ps(f"p_t{i}", [P, 4, P]) for i in range(n_tab)]
    s_rec, s_ch, s_tab, s_tr, s_out, s_st = (ph.sem(x) for x in ("rec", "chain", "tables", "T", "out", "stored"))

    with ph.block() as block:
        @block.gpsimd
        def _(pool):
            for k, piece in pieces:
                pool.indirect_dma_start(out=rec[:, piece, :].rearrange("p c f -> p (c f)"), out_offset=None,
                                        in_=lay.rec[:, :],
                                        in_offset=bass.IndirectOffsetOnAxis(ap=lay.off_i[0:G, k:k + 1], axis=0))\
                    .then_inc(s_rec, 16)

        @block.vector
        def _(dve):
            ch = Chain(dve, s_ch)
            f = lambda i: rec[:, :, i:i + 1].rearrange("p c f -> p (c f)")
            dve.wait_ge(s_rec, 16 * lay.per)
            for k, piece in pieces:
                ch(nc.vector.tensor_scalar(valid[:, piece], K.iota_row[0:G, 0:S], lay.grp[0:G, 0, k:k + 1],
                                           lay.grp[0:G, 1, k:k + 1], ALU.add, ALU.is_lt))

            def place(row, key):
                for k, piece in pieces:
                    ch(nc.vector.tensor_scalar(row[:, piece], key[:, piece], lay.grp[0:G, 2, k:k + 1], 1.0,
                                               ALU.subtract, ALU.add))
                ch(nc.vector.tensor_tensor(row, row, valid[:, :], ALU.mult))
                ch(nc.vector.tensor_scalar(row, row, 1.0, None, ALU.subtract))

            if not typed:
                ch(nc.vector.tensor_tensor(tab[:, SRC, :], f(0), valid[:, :], ALU.mult))
            if typed:
                ch(nc.vector.scalar_tensor_tensor(tab[:, 0, :], f(0), 8.0, f(2), ALU.mult, ALU.add))
                place(tab[:, 1, :], f(1))
                nc.vector.tensor_tensor(tab[:, 0, :], tab[:, 0, :], valid[:, :], ALU.mult).then_inc(s_tab, 1)
            elif by_dst:
                ch(nc.vector.scalar_tensor_tensor(tab[:, IDX3, :], f(0), 8.0, f(2), ALU.mult, ALU.add))
                ch(nc.vector.tensor_tensor(tab[:, IDX3, :], tab[:, IDX3, :], valid[:, :], ALU.mult))
                place(tab[:, DL, :], f(1))
                nc.vector.tensor_copy(dl_bf[:, :], tab[:, DL, :])
                nc.vector.tensor_copy(tab[:, W, :], f(3))
                for a in range(3):
                    nc.vector.tensor_copy(att[:, a, :], f(4 + a))
                ch(nc.vector.tensor_copy(tmp_i[:, 0, :], tab[:, SRC, :]))
                ch(nc.vector.tensor_scalar(tmp_i[:, 1, :], tmp_i[:, 0, :], P - 1, None, ALU.bitwise_and))
                ch(nc.vector.tensor_copy(tab[:, SLOC, :], tmp_i[:, 1, :]))
                ch(nc.vector.tensor_tensor(tab[:, COMB, :], tab[:, SRC, :], tab[:, SLOC, :], ALU.subtract))
                nc.vector.scalar_tensor_tensor(tab[:, COMB, :], tab[:, COMB, :], -float(NT * P // 2),
                                               tab[:, DL, :], ALU.add, ALU.add).then_inc(s_tab, 1)
            else:
                place(tab[:, 1, :], f(1))
                nc.vector.tensor_copy(tab[:, 2, :], f(2)).then_inc(s_tab, 1)
            for i in range(n_tab):
                dve.wait_ge(s_tr, i + 1)
                nc.vector.tensor_copy(out[:, i, :].rearrange("p (g k) -> p k g", k=4), p_t[i][:, :, 0:G])\
                  .then_inc(s_out, 1)

        @block.tensor
        def _(pe):
            pe.wait_ge(s_tab, 1)
            for i in range(n_tab):
                for k in range(4):
                    ins = nc.tensor.transpose(p_t[i][:, k, 0:G], tab[:, i, k * P:(k + 1) * P], K.ident[0:G, 0:G])
                ins.then_inc(s_tr, 1)

        @block.sync
        def _(sp):
            sp.wait_ge(s_tab, 1)
            if by_dst and not typed:
                sp.dma_start(dr.attT.rearrange("a (g c) -> g a c", c=GS), att[:, :, :]).then_inc(s_st, 16)
                sp.dma_start(dr.dlrow.rearrange("a (g c) -> (a g) c", c=GS), dl_bf[:, :]).then_inc(s_st, 16)
            sp.wait_ge(s_out, n_tab)
            sp.dma_start(lay.tabs[:, :], out[:, :, :].rearrange("p i c -> p (i c)")).then_inc(s_st, 16)
            sp.wait_ge(s_st, 48 if by_dst and not typed else 16)
    ph.close()


class Turn:

    def __init__(self, t, par, use, first):
        self.t, self.par, self.use, self.first = t, par, use, first


def pipelined(eng, n, *stages, order=None):
    depth = len(stages) - 1
    lead = depth + 2 + depth % 2
    loops = (n - lead) // 2
    order = order or range(len(stages))

    def turn(s):
        for i in order:
            if stages[i] is not None and 0 <= s - i < n:
                stages[i](Turn(s - i, (s - i) % 2, (s - i) // 2, s - i < 2))

    for s in range(lead):
        turn(s)
    with eng.Fori(0, loops) as j:
        for q in range(2):
            for i in order:
                if stages[i] is not None:
                    at = lead + q - i
                    stages[i](Turn(j * 2 + at, at % 2, j + at // 2, False))
    for s in range(lead + 2 * loops, n + depth):
        turn(s)


def broadcast_row(sp, tile, vec, sem):
    sp.dma_start(tile, vec.rearrange("(a d) -> a d", a=1).to_broadcast([P, D])).then_inc(sem, 16)


def column(sp, tile, vec, sem):
    sp.dma_start(tile, vec.rearrange("(d a) -> d a", a=1)).then_inc(sem, 16)


def node_norm(nc, ph, x, h, relu=True):
    mean = ph.sb("ln_mean", [P, NW])
    var = ph.sb("ln_var", [P, NW])
    sq = ph.sb("ln_sq", [P, NW, D])
    s_ch, s_ctr, s_sq, s_var, s_rstd, s_done = (ph.sem("ln_" + x) for x in (
        "chain", "centred", "squared", "var", "rstd", "done"))

    def wide(v):
        return v[:, :].unsqueeze(2).to_broadcast([P, NW, D])

    def vector(dve):
        ch = Chain(dve, s_ch)
        ch(nc.vector.tensor_reduce(mean[:, :], x[:, :, :], AX, ALU.add))
        ch(nc.vector.tensor_scalar(mean[:, :], mean[:, :], -1.0 / D, None, ALU.mult))
        nc.vector.tensor_tensor(h[:, :, :], x[:, :, :], wide(mean), ALU.add).then_inc(s_ctr, 1)
        dve.wait_ge(s_sq, 1)
        ch(nc.vector.tensor_reduce(var[:, :], sq[:, :, :], AX, ALU.add))
        nc.vector.tensor_scalar(var[:, :], var[:, :], 1.0 / D, LN_EPS, ALU.mult, ALU.add).then_inc(s_var, 1)
        dve.wait_ge(s_rstd, 1)
        dve.wait_ge(s_ctr, 1)
        if relu:
            ins = nc.vector.scalar_tensor_tensor(h[:, :, :], h[:, :, :], 0.0, wide(var), ALU.max, ALU.mult)
        else:
            ins = nc.vector.tensor_tensor(h[:, :, :], h[:, :, :], wide(var), ALU.mult)
        ins.then_inc(s_done, 1)

    def scalar(act):
        act.wait_ge(s_ctr, 1)
        nc.scalar.activation(sq[:, :, :], h[:, :, :], ACT.Square).then_inc(s_sq, 1)

    def gpsimd(pool, K):
        pool.wait_ge(s_var, 1)
        nc.gpsimd.tensor_tensor(var[:, :], var[:, :], K.neghalf[:, 0:NW], ALU.pow).then_inc(s_rstd, 1)

    return vector, scalar, gpsimd, s_done


def node_products(nc, ph, K, h, s_h, n_h, weights, width, outs, bias=None, parts=False):
    hT = [ph.sb(f"np_hT{i}", [P, P]) for i in range(2)]
    row = [ph.sb(f"np_row{i}", [P, width]) for i in range(2)]
    p_t = [ph.ps(f"np_pT{i}", [P, 512]) for i in range(2)]
    p_o = [ph.ps(f"np_pO{i}", [P, max(width, 512)]) for i in range(2)]
    s_t, s_hT, s_o, s_row = (ph.sem("np_" + x) for x in ("T", "hT", "product", "row"))
    s_st = [ph.sem(f"np_stored{i}") for i in range(2)]
    row3 = [ph.sb(f"np_row3{i}", [P, 3, D], BF16) for i in range(2)] if parts else row
    rest = ph.sb("np_rest", [P, D]) if parts else None
    s_ch = ph.sem("np_chain")
    n_out = len(outs(0, row[0], row3[0]))

    def tensor(pe):
        pe.wait_ge(s_h, n_h)
        for t in range(NT + 1):
            if t < NT:
                if t >= 2:
                    pe.wait_ge(s_hT, t - 1)
                nc.tensor.transpose(p_t[t % 2][:, 0:P], h[:, t, :], K.ident[:, :]).then_inc(s_t, 1)
            if t >= 1:
                u = t - 1
                pe.wait_ge(s_hT, u + 1)
                if u >= 2:
                    pe.wait_ge(s_row, u - 1)
                for b in range(0, width, 512):
                    e = min(b + 512, width)
                    ins = nc.tensor.matmul(p_o[u % 2][:, b:e], hT[u % 2][:, :], weights[:, b:e],
                                           start=True, stop=True)
                ins.then_inc(s_o, 1)

    def scalar(act):
        for t in range(NT):
            act.wait_ge(s_t, t + 1)
            if t >= 2:
                act.wait_ge(s_o, t - 1)
            nc.scalar.activation(hT[t % 2][:, :], p_t[t % 2][:, 0:P], ACT.Copy).then_inc(s_hT, 1)

    def vector(dve):
        ch = Chain(dve, s_ch)
        for t in range(NT):
            dve.wait_ge(s_o, t + 1)
            if t >= 2:
                dve.wait_ge(s_st[t % 2], t // 2 * 16 * n_out)
            if parts:
                nc.vector.tensor_copy(row[t % 2][:, D:width], p_o[t % 2][:, D:width])
                ins = split3(nc, ch, [row3[t % 2][:, i, :] for i in range(3)], p_o[t % 2][:, 0:D], rest[:, :])
            elif bias is None:
                ins = nc.vector.tensor_copy(row[t % 2][:, :], p_o[t % 2][:, 0:width])
            else:
                ins = nc.vector.tensor_tensor(row[t % 2][:, :], p_o[t % 2][:, 0:width], bias, ALU.add)
            ins.then_inc(s_row, 1)

    def sync(sp):
        for t in range(NT):
            sp.wait_ge(s_row, t + 1)
            for dst, part in outs(t, row[t % 2], row3[t % 2]):
                sp.dma_start(dst, part).then_inc(s_st[t % 2], 16)
        sp.wait_ge(s_st[0], (NT + 1) // 2 * 16 * n_out)
        sp.wait_ge(s_st[1], NT // 2 * 16 * n_out)

    return tensor, scalar, vector, sync


def start_nodes(nc, A, K, dr):
    ph = Phase(nc, "start")
    x = ph.sb("x", [P, NW, D])
    h = ph.sb("h", [P, NW, D])
    x0 = ph.sb("x0", [P, NW, D])
    w = ph.sb("w", [P, D])
    s_ld, s_z, s_x0, s_share, s_st = (ph.sem(v) for v in ("loaded", "zeroed", "x0", "share", "stored"))
    ln_v, ln_s, ln_g, s_ln = node_norm(nc, ph, x, h)
    np_t, np_s, np_v, np_sp = node_products(
        nc, ph, K, x0, s_x0, 1, w, D, lambda t, row, row3: [(dr.x0w[:, t * D:(t + 1) * D], row[:, :])])
    with ph.block() as block:
        @block.sync
        def _(sp):
            sp.wait_ge(s_z, 1)
            load_nodes(sp, x, A["x"], s_ld)
            sp.dma_start(w[:, :], A["L0_gnn_W2"][D:2 * D, :]).then_inc(s_ld, 16)
            sp.wait_ge(s_x0, 1)
            sp.dma_start(dr.x0[:, :], x0[:, 0:NT, :].rearrange("p t d -> p (t d)")).then_inc(s_st, 16)
            sp.wait_ge(s_share, 1)
            sp.dma_start(dr.x0share[:, :], h[:, 0:NT, :].rearrange("p t d -> p (t d)")).then_inc(s_st, 16)
            np_sp(sp)
            sp.wait_ge(s_st, 32)

        @block.gpsimd
        def _(pool):
            ln_g(pool, K)

        @block.scalar
        def _(act):
            ln_s(act)
            act.wait_ge(s_ln, 1)
            nc.scalar.activation(x0[:, :, :], h[:, :, :], ACT.Tanh).then_inc(s_x0, 1)
            np_s(act)

        @block.vector
        def _(dve):
            nc.vector.memset(x[:, NT - 1:NW, :], 0.0).then_inc(s_z, 1)
            dve.wait_ge(s_ld, 64)
            ln_v(dve)
            dve.wait_ge(s_x0, 1)
            nc.vector.tensor_scalar(h[:, :, :], x0[:, :, :], ALPHA, None, ALU.mult).then_inc(s_share, 1)
            np_v(dve)

        @block.tensor
        def _(pe):
            pe.wait_ge(s_ld, 64)
            np_t(pe)
    ph.close()


def split3(nc, ch, parts, src, tmp):
    ch(nc.vector.tensor_copy(parts[0], src))
    ch(nc.vector.tensor_tensor(tmp, src, parts[0], ALU.subtract))
    ch(nc.vector.tensor_copy(parts[1], tmp))
    return nc.vector.tensor_tensor(parts[2], tmp, parts[1], ALU.subtract)


def fuse_weights(nc, A, K, dr):
    ph = Phase(nc, "fuse")
    w1 = ph.sb("w1", [P, D])
    w1T = ph.sb("w1T", [P, D])
    w2 = ph.sb("w2", [P, D])
    b1 = ph.sb("b1", [P, 1])
    p_w = ph.ps("p_w", [P, 512])
    p_t = ph.ps("p_t", [P, 512])
    p_b = ph.ps("p_b", [P, 512])
    s_ld, s_t, s_tc, s_w = (ph.sem(v) for v in ("loaded", "T", "T_out", "products"))
    with ph.block() as block:
        @block.sync
        def _(sp):
            sp.dma_start(w1[:, :], A["L0_gnn_W1"]).then_inc(s_ld, 16)
            sp.dma_start(w2[:, :], A["L0_gnn_W2"][0:D, :]).then_inc(s_ld, 16)
            column(sp, b1[:, :], A["L0_gnn_b1"], s_ld)
            sp.dma_start(K.eps[:, 0:1], A["L0_gnn_eps1"].rearrange("(a d) -> a d", a=1).to_broadcast([P, 1])).then_inc(s_ld, 16)
            sp.dma_start(K.eps[:, 1:2], A["L0_gnn_eps2"].rearrange("(a d) -> a d", a=1).to_broadcast([P, 1])).then_inc(s_ld, 16)

        @block.tensor
        def _(pe):
            pe.wait_ge(s_ld, 80)
            nc.tensor.transpose(p_t[:, 0:D], w1[:, :], K.ident[:, :]).then_inc(s_t, 1)
            nc.tensor.matmul(p_b[0:1, 0:D], b1[:, :], w2[:, :], start=True, stop=True)
            pe.wait_ge(s_tc, 1)
            nc.tensor.matmul(p_w[:, 0:D], w1T[:, :], w2[:, :], start=True, stop=True).then_inc(s_w, 1)

        @block.vector
        def _(dve):
            dve.wait_ge(s_ld, 80)
            nc.vector.tensor_scalar(K.eps[:, :], K.eps[:, :], 1.0, None, ALU.add)
            dve.wait_ge(s_t, 1)
            nc.vector.tensor_copy(w1T[:, :], p_t[:, 0:D]).then_inc(s_tc, 1)
            dve.wait_ge(s_w, 1)
            nc.vector.tensor_copy(K.w12[:, :], p_w[:, 0:D])
            nc.vector.tensor_copy(K.b12[:, :], p_b[0:1, 0:D])
    ph.close()


def hops(nc, K, dr):
    ph = Phase(nc, "hop")
    h3 = [ph.sb(f"h3_{i}", [P, NT, 3, D], BF16) for i in range(2)]
    got = [ph.sb(f"got{i}", [P, 3, D]) for i in range(2)]
    side = [ph.sb(f"side{i}", [P, D]) for i in range(2)]
    h = ph.sb("h", [P, D])
    tmp = ph.sb("tmp", [P, D])
    z = [ph.sb(f"z{i}", [P, D]) for i in range(2)]
    zT = [ph.sb(f"zT{i}", [P, D]) for i in range(2)]
    p_a = [ph.ps(f"p_a{i}", [P, 512]) for i in range(2)]
    p_t = [ph.ps(f"p_t{i}", [P, 512]) for i in range(2)]
    p_y = [ph.ps(f"p_y{i}", [P, 512]) for i in range(2)]
    s_split, s_sum, s_got, s_ch = (ph.sem(v) for v in ("split", "summed", "got", "chain"))
    s_side = [ph.sem(f"side{i}") for i in range(2)]
    s_z, s_t, s_zT, s_y, s_a2, s_ch2 = (ph.sem(v) for v in ("z", "T", "zT", "y", "gin_sum", "gin_chain"))
    s_o = [ph.sem(f"o_stored{i}") for i in range(2)]
    s_oc = ph.sem("o")
    EVEN, ODD = (NT + 1) // 2, NT // 2
    ROUND = (EVEN, ODD)

    def loads(r):
        return dr.x0 if r == 0 else dr.x0share if r <= HOPS else dr.x0w

    with ph.block() as block:
        @block.sync
        def _(sp):
            for r in range(HOPS + 2):
                def load(u, r=r):
                    if not u.first:
                        sp.wait_ge(s_split, r * NT + u.t - 1)
                    elif r > 0:
                        sp.wait_ge(s_split, r * NT)
                    sp.dma_start(side[u.par][:, :], loads(r)[:, bass.ds(u.t * D, D)]).then_inc(s_side[u.par], 16)
                pipelined(sp, NT, load)

            def store(u):
                sp.wait_ge(s_oc, u.t + 1)
                sp.dma_start(dr.o[:, bass.ds(u.t * D, D)], z[u.par][:, :]).then_inc(s_o[u.par], 16)
            pipelined(sp, NT, store)
            sp.wait_ge(s_o[0], EVEN * 16)
            sp.wait_ge(s_o[1], ODD * 16)

        @block.tensor
        def _(pe):
            def products(u, src):
                for s in range(NT):
                    ins = nc.tensor.matmul(p_a[u.par][:, 0:3 * D], K.adj[:, s, bass.ds(u.t * P, P)],
                                           src[:, s, :, :].rearrange("p i d -> p (i d)"),
                                           start=(s == 0), stop=(s == NT - 1))
                ins.then_inc(s_sum, 1)

            for r in range(HOPS):
                pe.wait_ge(s_split, (r + 1) * NT)

                def hop(u, r=r):
                    if not u.first:
                        pe.wait_ge(s_got, r * NT + u.t - 1)
                    elif r > 0:
                        pe.wait_ge(s_got, r * NT)
                    products(u, h3[r % 2])
                pipelined(pe, NT, hop)
            pe.wait_ge(s_split, (HOPS + 1) * NT)

            def gin(u):
                if not u.first:
                    pe.wait_ge(s_a2, u.t - 1)
                else:
                    pe.wait_ge(s_got, HOPS * NT)
                products(u, h3[HOPS % 2])

            def turned(u):
                pe.wait_ge(s_z, u.t + 1)
                if not u.first:
                    pe.wait_ge(s_zT, u.t - 1)
                nc.tensor.transpose(p_t[u.par][:, 0:D], z[u.par][:, :], K.ident[:, :]).then_inc(s_t, 1)

            def weigh(u):
                pe.wait_ge(s_zT, u.t + 1)
                if not u.first:
                    pe.wait_ge(s_split, (HOPS + 1) * NT + u.t - 1)
                nc.tensor.matmul(p_y[u.par][:, 0:D], K.ones[0:1, :], K.b12[:, :], start=True, stop=False)
                nc.tensor.matmul(p_y[u.par][:, 0:D], zT[u.par][:, :], K.w12[:, :], start=False, stop=True)\
                    .then_inc(s_y, 1)
            pipelined(pe, NT, gin, turned, weigh)
            pe.wait_ge(s_split, (HOPS + 2) * NT)
            pe.wait_ge(s_a2, NT)

            def gin2(u):
                if not u.first:
                    pe.wait_ge(s_a2, NT + u.t - 1)
                products(u, h3[(HOPS + 1) % 2])
            pipelined(pe, NT, gin2)

        @block.scalar
        def _(act):
            for r in range(HOPS):
                def take(u, r=r):
                    act.wait_ge(s_sum, r * NT + u.t + 1)
                    if not u.first:
                        act.wait_ge(s_split, (r + 1) * NT + u.t - 1)
                    else:
                        act.wait_ge(s_split, (r + 1) * NT)
                    nc.scalar.activation(got[u.par][:, :, :].rearrange("p i d -> p (i d)"),
                                         p_a[u.par][:, 0:3 * D], ACT.Copy).then_inc(s_got, 1)
                pipelined(act, NT, take)

            def take_T(u):
                act.wait_ge(s_t, u.t + 1)
                if not u.first:
                    act.wait_ge(s_y, u.t - 1)
                nc.scalar.activation(zT[u.par][:, :], p_t[u.par][:, 0:D], ACT.Copy).then_inc(s_zT, 1)
            pipelined(act, NT, take_T)

        @block.vector
        def _(dve):
            ch = Chain(dve, s_ch)

            def split(r, u):
                split3(nc, ch, [h3[r % 2][:, bass.ds(u.t, 1), i, :].rearrange("p a d -> p (a d)")
                                for i in range(3)], h[:, :], tmp[:, :]).then_inc(s_split, 1)
                dve.wait_ge(s_split, r * NT + u.t + 1)

            def start(u):
                ch.turn(u.t * 4)
                dve.wait_ge(s_side[u.par], (u.use + 1) * 16)
                ch(nc.vector.tensor_scalar(h[:, :], side[u.par][:, :], K.norm[:, 1, bass.ds(u.t, 1)], None, ALU.mult))
                split(0, u)
            pipelined(dve, NT, start)
            before = 4 * NT
            for r in range(1, HOPS + 1):
                last = r == HOPS
                ops = 6 if last else 7

                def hop(u, r=r, last=last, ops=ops, before=before):
                    ch.turn(u.t * ops + before)
                    g = got[u.par]
                    dve.wait_ge(s_got, (r - 1) * NT + u.t + 1)
                    dve.wait_ge(s_side[u.par], (ROUND[u.par] * r + u.use + 1) * 16)
                    ch(nc.vector.tensor_tensor(tmp[:, :], g[:, 1, :], g[:, 2, :], ALU.add))
                    ch(nc.vector.tensor_tensor(tmp[:, :], tmp[:, :], g[:, 0, :], ALU.add))
                    ch(nc.vector.scalar_tensor_tensor(h[:, :], tmp[:, :], K.norm8[:, bass.ds(u.t, 1)],
                                                      side[u.par][:, :], ALU.mult, ALU.add))
                    if not last:
                        ch(nc.vector.tensor_scalar(h[:, :], h[:, :], K.norm[:, 1, bass.ds(u.t, 1)], None, ALU.mult))
                    split(r, u)
                pipelined(dve, NT, hop)
                before += ops * NT

            ch2 = Chain(dve, s_ch2)

            def gin_sum(u, which, eps):
                g = got[u.par]
                ch2.turn(u.t + which * NT)
                nc.vector.scalar_tensor_tensor(
                    g[:, :, :].rearrange("p i d -> p (i d)"),
                    h3[(HOPS + which) % 2][:, bass.ds(u.t, 1), :, :].rearrange("p a i d -> p (a i d)"), eps,
                    p_a[u.par][:, 0:3 * D], ALU.mult, ALU.add).then_inc(s_a2, 1)
                dve.wait_ge(s_a2, which * NT + u.t + 1)
                ch2(nc.vector.tensor_tensor(g[:, 1, :], g[:, 1, :], g[:, 2, :], ALU.add))
                return nc.vector.tensor_tensor(z[u.par][:, :], g[:, 1, :], g[:, 0, :], ALU.add)

            def gin_a(u):
                dve.wait_ge(s_sum, HOPS * NT + u.t + 1)
                if not u.first:
                    dve.wait_ge(s_t, u.t - 1)
                gin_sum(u, 0, K.eps[:, 0:1]).then_inc(s_z, 1)

            def gin_b(u, before=before):
                ch.turn(u.t * 4 + before)
                dve.wait_ge(s_y, u.t + 1)
                dve.wait_ge(s_side[u.par], (ROUND[u.par] * (HOPS + 1) + u.use + 1) * 16)
                ch(nc.vector.tensor_tensor(h[:, :], p_y[u.par][:, 0:D], side[u.par][:, :], ALU.add))
                split(HOPS + 1, u)
            pipelined(dve, NT, gin_a, None, gin_b)

            def gin2(u):
                dve.wait_ge(s_sum, (HOPS + 1) * NT + u.t + 1)
                if not u.first:
                    dve.wait_ge(s_o[u.par], u.use * 16)
                gin_sum(u, 1, K.eps[:, 1:2]).then_inc(s_oc, 1)
            dve.wait_ge(s_t, NT)
            pipelined(dve, NT, gin2)
    ph.close()


def adjacency(nc, K, dr):
    ph = Phase(nc, "adj")
    W = NT * P
    BANK = 512
    PIECE = 2 * BANK
    VB, VE = PIECE, 2 * PIECE
    PIECES = (W + PIECE - 1) // PIECE - 1
    HALF = 3 * BANK
    OD = 10
    lay = dr.by_dst
    side_idx = [ph.sb(f"side_idx{i}", [EP, 1], I32) for i in range(2)]
    side_rec = [ph.sb(f"side_rec{i}", [EP, REC2]) for i in range(2)]
    s_side, s_copied, s_turn = [ph.sem(f"side{i}") for i in range(2)], ph.sem("side_copied"), ph.sem("turn")
    rank2 = ph.sb("rank2", [EP, EC], I32)
    rec2 = ph.sb("rec2", [EP, EC, REC2])
    s_rank = ph.sem("ranks")
    tabs = ph.sb("tabs", [P, 2, G * 4])
    iota = ph.sb("iota", [P, W], FP16)
    comb = [ph.sb(f"comb{i}", [P, W], BF16) for i in range(2)]
    sloc = [ph.sb(f"sloc{i}", [P, P], BF16) for i in range(4)]
    iota_p = ph.sb("iota_row16", [P, P], FP16)
    ident = ph.sb("ident_bf", [P, P], BF16)
    acc = ph.ps("acc", [P, W])
    dg = ph.ps("deg", [P, 32])
    s_tab, s_iota, s_hot, s_chunk, s_bank, s_out, s_z, s_deg, s_ch, s_id, s_od, s_hot2, s_half, s_vout = (ph.sem(x) for x in (
        "tables", "iotas", "onehots", "chunk", "bank_summed", "banks_out", "zeroed", "degree", "chain",
        "identity", "out_degrees", "onehots2", "half", "piece_out"))
    ZT = 17
    BANKS = (W + BANK - 1) // BANK

    with ph.block() as block:
        @block.sync
        def _(sp):
            sp.dma_start(tabs[:, :, :].rearrange("p i c -> p (i c)"), lay.tabs[:, 4 * G * 4:6 * G * 4]).then_inc(s_tab, 16)
            sp.dma_start(rank2[:, :], dr.by_src.rank[:, :]).then_inc(s_rank, 16)
            sp.dma_start(rec2[:, :, :].rearrange("p c f -> p (c f)"), dr.by_src.unsorted[:, :]).then_inc(s_rank, 16)

        @block.gpsimd
        def _(pool):
            nc.gpsimd.iota(iota[:, :], pattern=[[1, W]], base=-(W // 2), channel_multiplier=0,
                           allow_small_or_imprecise_dtypes=True)
            nc.gpsimd.iota(iota_p[:, :], pattern=[[1, P]], base=0, channel_multiplier=0,
                           allow_small_or_imprecise_dtypes=True).then_inc(s_iota, 1)
            nc.gpsimd.memset(K.adj[:, ZT:NT, :], 0.0).then_inc(s_z, 1)

            def send(u):
                if not u.first:
                    pool.wait_ge(s_side[u.par], u.use * 16)
                    pool.sem_inc(s_turn, 1)
                nc.gpsimd.tensor_copy(side_idx[u.par][:, :], rank2[:, bass.ds(u.t, 1)])
                nc.gpsimd.tensor_copy(side_rec[u.par][:, :], rec2[:, bass.ds(u.t, 1), :].rearrange("p a f -> p (a f)"))\
                    .then_inc(s_copied, 1)
                pool.wait_ge(s_copied, u.t + 1)
                pool.sem_inc(s_turn, 1)
                pool.indirect_dma_start(
                    out=dr.by_src.rec[:, :], out_offset=bass.IndirectOffsetOnAxis(ap=side_idx[u.par][:, 0:1], axis=0),
                    in_=side_rec[u.par][:, :], in_offset=None).then_inc(s_side[u.par], 16)
            pool.wait_ge(s_rank, 32)
            pipelined(pool, EC, send)
            for i in range(2):
                pool.wait_ge(s_side[i], EC // 2 * 16)

        @block.tensor
        def _(pe):
            def group(g, first):
                at = pe.value_load(lay.tile_row[0:1, bass.ds(g, 1)], min_val=0, max_val=(NT - 1) * P)
                for k in range(4):
                    for b in range(0, W, BANK):
                        if b == 0:
                            pe.wait_ge(s_hot, g * 4 + k + 1)
                        elif b == HALF:
                            pe.wait_ge(s_hot2, g * 4 + k + 1)
                        if k == 0 and not first:
                            if b == VB:
                                pe.wait_ge(s_vout, g)
                            elif b % PIECE == 0:
                                pe.wait_ge(s_out, (g - 1) * PIECES + b // PIECE + (1 if b < VB else 0))
                        e = min(b + BANK, W)
                        ins = nc.tensor.matmul(acc[:, b:e], sloc[k][:, :], comb[k % 2][:, b:e],
                                               start=(k == 0), stop=False)
                        if e == HALF:
                            ins.then_inc(s_half, 1)
                    ins.then_inc(s_chunk, 1)
                if first:
                    pe.wait_ge(s_z, 2)
                    pe.wait_ge(s_id, 1)
                for b in range(0, W, BANK):
                    e = min(b + BANK, W)
                    nc.tensor.matmul(acc[:, b:e].rearrange("p (s c) -> p s c", c=P), ident[:, :],
                                     K.adj[:, b // P:e // P, bass.ds(at, P)], start=False, stop=True)\
                        .then_inc(s_bank, 1)
            group(0, True)
            with pe.Fori(1, G) as g:
                group(g, False)
            pe.wait_ge(s_out, G * PIECES)
            pe.wait_ge(s_vout, G)
            for t in range(NT):
                for s in range(NT):
                    ins = nc.tensor.matmul(dg[:, t:t + 1], K.adj[:, s, t * P:(t + 1) * P], K.ones_bf[:, 0:1],
                                           start=(s == 0), stop=(s == NT - 1))
            ins.then_inc(s_deg, 1)

        @block.scalar
        def _(act):
            def group(g):
                at = act.value_load(lay.tile_row[0:1, bass.ds(g, 1)], min_val=0, max_val=(NT - 1) * P)
                for b in range(0, W, PIECE):
                    if b == VB:
                        continue
                    e = min(b + PIECE, W)
                    act.wait_ge(s_bank, g * BANKS + (e + BANK - 1) // BANK)
                    nc.scalar.activation(K.adj[:, b // P:e // P, bass.ds(at, P)],
                                         acc[:, b:e].rearrange("p (s c) -> p s c", c=P), ACT.Copy).then_inc(s_out, 1)
            group(0)
            with act.Fori(1, G) as g:
                group(g)
            act.wait_ge(s_out, G * PIECES)
            act.wait_ge(s_vout, G)
            for s in range(OD, NT):
                nc.scalar.activation(comb[s % 2][:, :], K.adj[:, s, :], ACT.Copy, accum_out=K.deg[:, 1, s:s + 1])\
                    .then_inc(s_od, 1)
                act.wait_ge(s_od, s - OD + 1)

        @block.vector
        def _(dve):
            ch = Chain(dve, s_ch)
            nc.vector.memset(K.adj[:, 0:ZT, :], 0.0).then_inc(s_z, 1)
            nc.vector.tensor_copy(ident[:, :], K.ident[:, :]).then_inc(s_id, 1)
            dve.wait_ge(s_tab, 16)
            dve.wait_ge(s_iota, 1)

            def onehots(g, k, first):
                again = not (first and k < 2)
                col = bass.ds(g * 4 + k, 1)
                if again:
                    dve.wait_ge(s_half, g * 4 + k - 1)
                nc.vector.tensor_scalar(sloc[k][:, :], iota_p[:, :], tabs[:, 0, col], None, ALU.is_equal)
                nc.vector.tensor_scalar(comb[k % 2][:, 0:HALF], iota[:, 0:HALF], tabs[:, 1, col], None, ALU.is_equal)\
                    .then_inc(s_hot, 1)
                if again:
                    dve.wait_ge(s_chunk, g * 4 + k - 1)
                nc.vector.tensor_scalar(comb[k % 2][:, HALF:W], iota[:, HALF:W], tabs[:, 1, col], None, ALU.is_equal)\
                    .then_inc(s_hot2, 1)

            for k in range(4):
                onehots(0, k, True)

            def take(g):
                at = dve.value_load(lay.tile_row[0:1, bass.ds(g, 1)], min_val=0, max_val=(NT - 1) * P)
                dve.wait_ge(s_bank, g * BANKS + VE // BANK)
                nc.vector.tensor_copy(K.adj[:, VB // P:VE // P, bass.ds(at, P)],
                                      acc[:, VB:VE].rearrange("p (s c) -> p s c", c=P)).then_inc(s_vout, 1)

            with dve.Fori(1, G) as g:
                onehots(g, 0, False)
                onehots(g, 1, False)
                take(g - 1)
                onehots(g, 2, False)
                onehots(g, 3, False)
            take(G - 1)
            dve.wait_ge(s_out, G * PIECES)
            dve.wait_ge(s_vout, G)
            for s in range(OD):
                nc.vector.tensor_reduce(K.deg[:, 1, s:s + 1], K.adj[:, s, :], AX, ALU.add)
            dve.wait_ge(s_od, NT - OD)
            dve.wait_ge(s_deg, 1)
            ch(nc.vector.tensor_copy(K.deg[:, 0, 0:NT], dg[:, 0:NT]))
            ch(nc.vector.tensor_scalar(K.norm[:, :, 0:NT], K.deg[:, :, 0:NT], 1.0, None, ALU.max))
            ch(nc.vector.memset(K.scr[:, 0:1], 0.0))
    ph.close()

    ph = Phase(nc, "pow")
    s_p = ph.sem("powers")
    with ph.block() as block:
        @block.gpsimd
        def _(pool):
            for i in range(2):
                nc.gpsimd.tensor_tensor(K.norm[:, i, 0:NT], K.norm[:, i, 0:NT], K.neghalf[:, 0:NT], ALU.pow)\
                    .then_inc(s_p, 1)

        @block.vector
        def _(dve):
            dve.wait_ge(s_p, 2)
            nc.vector.tensor_scalar(K.norm8[:, 0:NT], K.norm[:, 0, 0:NT], 1.0 - ALPHA, None, ALU.mult)
    ph.close()


def gnn_input(nc, A, K, dr):
    ph = Phase(nc, "mid")
    o = ph.sb("o", [P, NW, D])
    e = ph.sb("e", [P, NW, D])
    b2 = ph.sb("b2", [P, D])
    w = ph.sb("w", [P, 2 * D])
    s_z, s_ld, s_m, s_e, s_ch, s_x = (ph.sem(v) for v in ("zeroed", "loaded", "clipped", "exp", "chain", "x"))
    ln_v, ln_s, ln_g, s_ln = node_norm(nc, ph, K.x, K.h)
    np_t, np_s, np_v, np_sp = node_products(
        nc, ph, K, K.h, s_ln, 1, w, 2 * D,
        lambda t, row, row3: [(dr.near[t * P:(t + 1) * P, :], row3[:, :, :].rearrange("p i d -> p (i d)")),
                              (dr.far[t * P:(t + 1) * P, :], row[:, D:2 * D])], parts=True)
    with ph.block() as block:
        @block.sync
        def _(sp):
            sp.wait_ge(s_z, 1)
            load_nodes(sp, K.x, A["x"], s_ld)
            sp.dma_start(o[:, 0:NT, :].rearrange("p t d -> p (t d)"), dr.o[:, :]).then_inc(s_ld, 16)
            broadcast_row(sp, b2[:, :], A["L0_gnn_b2"], s_ld)
            for i in range(2):
                sp.dma_start(w[:, i * D:(i + 1) * D], A["L1_gnn_eW1"][0, i * D:(i + 1) * D, :]).then_inc(s_ld, 16)
            np_sp(sp)

        @block.gpsimd
        def _(pool):
            ln_g(pool, K)

        @block.scalar
        def _(act):
            act.wait_ge(s_m, 1)
            nc.scalar.activation(e[:, :, :], e[:, :, :], ACT.Exp).then_inc(s_e, 1)
            ln_s(act)
            np_s(act)

        @block.tensor
        def _(pe):
            np_t(pe)

        @block.vector
        def _(dve):
            ch = Chain(dve, s_ch)
            nc.vector.memset(o[:, NT:NW, :], 0.0)
            nc.vector.memset(K.x[:, NT - 1:NW, :], 0.0).then_inc(s_z, 1)
            dve.wait_ge(s_ld, 112)
            ch(nc.vector.tensor_tensor(o[:, :, :], o[:, :, :], b2[:, :].unsqueeze(1).to_broadcast([P, NW, D]), ALU.add))
            nc.vector.tensor_scalar(e[:, :, :], o[:, :, :], 20.0, None, ALU.min).then_inc(s_m, 1)
            dve.wait_ge(s_e, 1)
            ch(nc.vector.scalar_tensor_tensor(e[:, :, :], e[:, :, :], 2.0, e[:, :, :], ALU.add, ALU.mult))
            ch(nc.vector.tensor_tensor(o[:, :, :], o[:, :, :], e[:, :, :], ALU.mult))
            ch(nc.vector.tensor_scalar(e[:, :, :], e[:, :, :], 2.0, None, ALU.add))
            ch(nc.vector.reciprocal(e[:, :, :], e[:, :, :]))
            ch(nc.vector.tensor_tensor(o[:, :, :], o[:, :, :], e[:, :, :], ALU.mult))
            ch(nc.vector.tensor_tensor(K.x[:, :, :], K.x[:, :, :], o[:, :, :], ALU.add))
            ln_v(dve)
            np_v(dve)
    ph.close()


EMBED, LAYER0, LAYER1 = range(3)


def edge_pass(nc, A, K, dr, kind):
    ph = Phase(nc, ("emb", "la", "lb")[kind])
    layer = kind - 1
    emb = kind == EMBED
    keeps = kind != LAYER1
    lay = dr.by_dst
    if emb:
        W1, b1, W2, b2, g, beta = (A["L1_gnn_emb_" + v] for v in ("W1", "b1", "W2", "b2", "g", "beta"))
    else:
        W1, b1, W2, b2, g, beta = (A["L1_gnn_" + v][layer] for v in ("eW1", "eb1", "eW2", "eb2", "eg", "ebeta"))
        W1 = W1[2 * D:3 * D, :]
    KIN = 3 if emb else P

    def two(name, shape, dt=F32):
        return [ph.sb(f"{name}{i}", shape, dt) for i in range(2)]

    w1 = ph.sb("w1", [KIN, D])
    w2 = ph.sb("w2", [P, D])
    col = ph.sb("col", [P, 3])
    g_row = ph.sb("g_row", [P, D])
    beta_row = ph.sb("beta_row", [P, D])
    b2x3 = ph.sb("b2x3", [3, D])
    b2p = ph.sb("b2p", [3, 3, D])
    b2h = ph.sb("b2h", [3, 3, D], BF16)
    b2r = ph.sb("b2r", [3, 4, D], BF16)
    tabs = ph.sb("tabs", [P, 3, G * 4])
    feat = two("feat", [KIN, GS])
    if not emb:
        place = two("place", [P, GS], BF16)
        spread = two("spread", [P, GS], BF16)
        near = two("near", [P, 3 * D], BF16)
        idx = two("idx", [P, 4], I32)
        far = two("far", [P, 4, D])
    hid = two("hid", [P, GS])
    s = two("s", [P, 4, D])
    stats = two("stats", [P, 4, 6])
    mv = two("mv", [P, 4, 2])
    ve = two("ve", [P, 4])
    n = two("n", [P, 4, D])
    hot = two("hot", [P, 4, P])
    if keeps:
        out = two("out", [P, GS])
    if kind == LAYER0:
        feat2 = two("feat2", [P, GS])
        scaled = two("scaled", [P, GS])
        s_scaled = ph.sem("scaled")
    p_z = [ph.ps(f"p_z{i}", [P, GS]) for i in range(2)]
    p_m = [ph.ps(f"p_m{i}", [P, 4, D]) for i in range(2)]
    p_n = [ph.ps(f"p_n{i}", [P, GS]) for i in range(2)]
    p_s = [ph.ps(f"p_s{i}", [P, 512]) for i in range(2)]
    (s_w, s_b2, s_zero, s_spread, s_idx, s_turn, s_z, s_hid, s_m, s_s, s_var, s_rstd, s_n, s_nT, s_sum, s_out,
     s_add, s_ch, s_end, s_stats) = (ph.sem(v) for v in (
         "weights", "b2_parts", "zeroed", "spread", "idx", "turn", "z", "hidden", "m", "s", "var", "rstd", "n", "nT",
         "sums", "out", "added", "moments", "end", "stats"))
    s_feat, s_feat2, s_far, s_st = ([ph.sem(f"{v}{i}") for i in range(2)] for v in ("feat", "feat2", "far", "stored"))
    n_feat = 16 if emb else 48
    EVEN, ODD = (G + 1) // 2, G // 2

    with ph.block() as block:
        @block.sync
        def _(sp):
            sp.dma_start(w1[:, :], W1).then_inc(s_w, 16)
            sp.dma_start(w2[:, :], W2).then_inc(s_w, 16)
            for i, v in enumerate((b1, g, beta)):
                column(sp, col[:, i:i + 1], v, s_w)
            broadcast_row(sp, g_row[:, :], g, s_w)
            broadcast_row(sp, beta_row[:, :], beta, s_w)
            sp.dma_start(b2x3[:, :], b2.rearrange("(a d) -> a d", a=1).to_broadcast([3, D])).then_inc(s_w, 16)
            sp.dma_start(tabs[:, :, :].rearrange("p i c -> p (i c)"), lay.tabs[:, 0:3 * G * 4]).then_inc(s_w, 16)

            def load(u):
                if not u.first:
                    sp.wait_ge(s_z, u.t - 1)
                cols = bass.ds(u.t * GS, GS)
                if emb:
                    sp.dma_start(feat[u.par][:, :], dr.attT[:, cols]).then_inc(s_feat[u.par], 16)
                    return
                at = sp.value_load(lay.tile_row[0:1, bass.ds(u.t, 1)], min_val=0, max_val=(NT - 1) * P)
                sp.dma_start(near[u.par][:, :], dr.near[bass.ds(at, P), :]).then_inc(s_feat[u.par], 16)
                sp.dma_start(place[u.par][:, :], dr.dlrow[:, cols].to_broadcast([P, GS])).then_inc(s_feat[u.par], 16)
                sp.dma_start(feat[u.par][:, :], dr.ea[layer][:, cols]).then_inc(s_feat[u.par], 16)

            def load_again(u):
                if not u.first:
                    sp.wait_ge(s_out, u.t - 1)
                sp.dma_start(feat2[u.par][:, :], dr.ea[layer][:, bass.ds(u.t * GS, GS)]).then_inc(s_feat2[u.par], 16)

            def store(u):
                sp.wait_ge(s_out, u.t + 1)
                sp.dma_start(dr.ea[kind][:, bass.ds(u.t * GS, GS)], out[u.par][:, :]).then_inc(s_st[u.par], 16)

            if emb:
                pipelined(sp, G, None, load, None, None, None, None, store)
            elif kind == LAYER0:
                pipelined(sp, G, None, load, None, None, load_again, None, store, order=(1, 4, 6))
            else:
                pipelined(sp, G, load)
            if keeps:
                sp.wait_ge(s_st[0], EVEN * 16)
                sp.wait_ge(s_st[1], ODD * 16)

        @block.gpsimd
        def _(pool):
            def gather(u):
                if not u.first:
                    pool.wait_ge(s_z, u.t - 1)
                pool.wait_ge(s_idx, u.t + 1)
                pool.sem_inc(s_turn, 1)
                for k in range(4):
                    pool.indirect_dma_start(out=far[u.par][:, k, :], out_offset=None, in_=dr.far[:, :],
                                            in_offset=bass.IndirectOffsetOnAxis(ap=idx[u.par][:, k:k + 1], axis=0))\
                        .then_inc(s_far[u.par], 16)

            def power(u):
                pool.wait_ge(s_var, u.t + 1)
                nc.gpsimd.tensor_tensor(ve[u.par][:, :], ve[u.par][:, :], K.neghalf[:, 0:4], ALU.pow)\
                    .then_inc(s_rstd, 1)
            if emb:
                pipelined(pool, G, power)
            else:
                pipelined(pool, G, None, gather, None, power, order=(1, 3))

        @block.tensor
        def _(pe):
            def first(u):
                if not u.first:
                    pe.wait_ge(s_hid, u.t - 1)
                if not emb:
                    pe.wait_ge(s_far[u.par], (u.use + 1) * 64)
                    for k in range(4):
                        nc.tensor.matmul(p_z[u.par][:, k * P:(k + 1) * P], far[u.par][:, k, :], K.ident[:, :],
                                         is_transpose=True, start=(k == 0), stop=False)
                    pe.wait_ge(s_feat[u.par], (u.use + 1) * n_feat)
                    pe.wait_ge(s_spread, u.t + 1)
                    for i in range(3):
                        nc.tensor.matmul(p_z[u.par][:, :], near[u.par][:, i * D:(i + 1) * D], spread[u.par][:, :],
                                         start=False, stop=False)
                else:
                    pe.wait_ge(s_feat[u.par], (u.use + 1) * n_feat)
                ins = nc.tensor.matmul(p_z[u.par][:, :], w1[:, :], feat[u.par][:, :], start=emb, stop=True)
                ins.then_inc(s_z, 1)

            def second(u):
                pe.wait_ge(s_hid, u.t + 1)
                if not u.first:
                    pe.wait_ge(s_s, u.t - 1)
                nc.tensor.matmul(p_m[u.par][:, :, :].rearrange("p k d -> p (k d)"), K.ones_bf[0:3, :],
                                 b2r[:, :, :].rearrange("p k d -> p (k d)"), start=True, stop=False)
                for k in range(4):
                    ins = nc.tensor.matmul(p_m[u.par][:, k, :], hid[u.par][:, k * P:(k + 1) * P], w2[:, :],
                                           start=False, stop=(k == 3))
                ins.then_inc(s_m, 1)

            def third(u):
                pe.wait_ge(s_n, u.t + 1)
                if not u.first:
                    pe.wait_ge(s_add, u.t - 1)
                if keeps:
                    if not u.first:
                        pe.wait_ge(s_out, u.t - 1)
                    for k in range(4):
                        ins = nc.tensor.transpose(p_n[u.par][:, k * P:(k + 1) * P], n[u.par][:, k, :], K.ident[:, :])
                    ins.then_inc(s_nT, 1)
                for k in range(4):
                    ins = nc.tensor.matmul(p_s[u.par][:, 0:D], hot[u.par][:, k, :], n[u.par][:, k, :],
                                           start=(k == 0), stop=(k == 3))
                ins.then_inc(s_sum, 1)
            pe.wait_ge(s_w, 144)
            pe.wait_ge(s_b2, 1)
            pipelined(pe, G, None, None, first, second, third, order=(3, 2, 4))

        @block.scalar
        def _(act):
            def hidden(u):
                act.wait_ge(s_z, u.t + 1)
                if not u.first:
                    act.wait_ge(s_m, u.t - 1)
                nc.scalar.activation(hid[u.par][:, :], p_z[u.par][:, :], ACT.Silu, bias=col[:, 0:1]).then_inc(s_hid, 1)

            def rows(u):
                act.wait_ge(s_m, u.t + 1)
                if not u.first:
                    act.wait_ge(s_n, u.t - 1)
                nc.scalar.activation(s[u.par][:, :, :].rearrange("p k d -> p (k d)"),
                                     p_m[u.par][:, :, :].rearrange("p k d -> p (k d)"), ACT.Silu).then_inc(s_s, 1)

            def scale(u):
                act.wait_ge(s_nT, u.t + 1)
                if emb:
                    if not u.first:
                        act.wait_ge(s_st[u.par], u.use * 16)
                    nc.scalar.activation(out[u.par][:, :], p_n[u.par][:, :], ACT.Identity, bias=col[:, 2:3],
                                         scale=col[:, 1:2]).then_inc(s_out, 1)
                else:
                    if not u.first:
                        act.wait_ge(s_out, u.t - 1)
                    nc.scalar.activation(scaled[u.par][:, :], p_n[u.par][:, :], ACT.Identity, bias=col[:, 2:3],
                                         scale=col[:, 1:2]).then_inc(s_scaled, 1)
            act.wait_ge(s_w, 144)
            if keeps:
                pipelined(act, G, None, None, hidden, rows, scale, order=(3, 2, 4))
            else:
                pipelined(act, G, None, None, hidden, rows, order=(3, 2))

        @block.vector
        def _(dve):
            ch0 = Chain(dve, s_zero)
            dve.wait_ge(s_w, 144)
            nc.vector.memset(K.sum[:, :, :], 0.0)
            ch0(nc.vector.tensor_copy(b2h[:, 0, :], b2x3[:, :]))
            ch0(nc.vector.tensor_tensor(b2p[:, 0, :], b2x3[:, :], b2h[:, 0, :], ALU.subtract))
            ch0(nc.vector.tensor_copy(b2h[:, 1, :], b2p[:, 0, :]))
            ch0(nc.vector.tensor_tensor(b2h[:, 2, :], b2p[:, 0, :], b2h[:, 1, :], ALU.subtract))
            ch0(nc.vector.tensor_scalar(b2p[:, 0, :], b2h[:, 0, :], K.ident[0:3, 0:1], None, ALU.mult))
            for i in range(1, 3):
                ch0(nc.vector.scalar_tensor_tensor(b2p[:, i, :], b2h[:, i, :], K.ident[0:3, i:i + 1], b2p[:, i - 1, :],
                                                   ALU.mult, ALU.add))
            for k in range(4):
                ins = nc.vector.tensor_copy(b2r[:, k, :], b2p[:, 2, :])
            ins.then_inc(s_b2, 1)

            def indices(u):
                if not u.first:
                    dve.wait_ge(s_far[u.par], u.use * 64)
                nc.vector.tensor_scalar(idx[u.par][:, :], tabs[:, 0, bass.ds(u.t * 4, 4)], 0.0, None, ALU.add)\
                    .then_inc(s_idx, 1)

            def place_hot(u):
                dve.wait_ge(s_feat[u.par], (u.use + 1) * n_feat)
                if not u.first:
                    dve.wait_ge(s_z, u.t - 1)
                nc.vector.tensor_scalar(spread[u.par][:, :], place[u.par][:, :], K.iota_p[:, 0:1], None, ALU.is_equal)\
                    .then_inc(s_spread, 1)

            def moments(u):
                dve.wait_ge(s_s, u.t + 1)
                for k in range(4):
                    ins = nc.vector.bn_stats(stats[u.par][:, k, :], s[u.par][:, k, :])
                ins.then_inc(s_stats, 1)
                if not u.first:
                    dve.wait_ge(s_sum, u.t - 1)

                def hots(ks):
                    for k in ks:
                        nc.vector.tensor_scalar(hot[u.par][:, k, :], K.iota_row[:, 0:P],
                                                tabs[:, 2, bass.ds(u.t * 4 + k, 1)], None, ALU.is_equal)
                hots([0, 1])
                dve.wait_ge(s_stats, u.t + 1)
                hots([2])
                for k in range(4):
                    ins = nc.vector.bn_aggr(mv[u.par][:, k, :], stats[u.par][:, k, :])
                ins.then_inc(s_ch, 1)
                hots([3])
                dve.wait_ge(s_ch, u.t + 1)
                nc.vector.tensor_scalar(ve[u.par][:, :], mv[u.par][:, :, 1:2].rearrange("p k a -> p (k a)"), LN_EPS,
                                        None, ALU.add).then_inc(s_var, 1)

            def norm(u):
                dve.wait_ge(s_rstd, u.t + 1)
                for k in range(4):
                    ins = nc.vector.tensor_scalar(n[u.par][:, k, :], s[u.par][:, k, :], mv[u.par][:, k, 0:1],
                                                  ve[u.par][:, k:k + 1], ALU.subtract, ALU.mult)
                ins.then_inc(s_n, 1)

            def add(u):
                if kind == LAYER0:
                    dve.wait_ge(s_scaled, u.t + 1)
                    dve.wait_ge(s_feat2[u.par], (u.use + 1) * 16)
                    if not u.first:
                        dve.wait_ge(s_st[u.par], u.use * 16)
                    nc.vector.tensor_tensor(out[u.par][:, :], scaled[u.par][:, :], feat2[u.par][:, :], ALU.add)\
                        .then_inc(s_out, 1)
                at = dve.value_load(lay.tile_row[0:1, bass.ds(u.t, 1)], min_val=0, max_val=(NT - 1) * P)
                dve.wait_ge(s_sum, u.t + 1)
                if not (isinstance(u.t, int) and u.t == 0):
                    dve.wait_ge(s_add, u.t)
                total = K.sum[:, :, :].rearrange("p t d -> p (t d)")[:, bass.ds(at, D)]
                nc.vector.tensor_tensor(total, p_s[u.par][:, 0:D], total, ALU.add).then_inc(s_add, 1)
            if emb:
                pipelined(dve, G, None, None, None, moments, norm, add, order=(4, 3, 5))
            else:
                pipelined(dve, G, indices, place_hot, None, moments, norm, add, order=(4, 0, 1, 3, 5))

            dve.wait_ge(s_add, G)
            che = Chain(dve, s_end)
            wide = lambda v: v[:, :].unsqueeze(1).to_broadcast([P, NW, D])
            che(nc.vector.tensor_tensor(K.sum[:, :, :], K.sum[:, :, :], wide(g_row), ALU.mult))
            if emb:
                che(nc.vector.tensor_copy(K.agg[:, :, :], K.sum[:, :, :]))
            else:
                che(nc.vector.tensor_tensor(K.agg[:, :, :], K.agg[:, :, :], K.sum[:, :, :], ALU.add))
            che(nc.vector.tensor_tensor(K.sum[:, :, :], wide(beta_row),
                                        K.deg[:, 0, :].unsqueeze(2).to_broadcast([P, NW, D]), ALU.mult))
            che(nc.vector.tensor_tensor(K.agg[:, :, :], K.agg[:, :, :], K.sum[:, :, :], ALU.add))
    ph.close()


def node_update(nc, A, K, dr, layer):
    ph = Phase(nc, f"node{layer}")
    W1, b1, W2, b2, g, beta = (A["L1_gnn_" + v][layer] for v in ("nW1", "nb1", "nW2", "nb2", "ng", "nbeta"))
    w1 = ph.sb("w1", [P, 2, D])
    w2 = ph.sb("w2", [P, D])
    wn = ph.sb("wn", [P, 2 * D])
    b1c = ph.sb("b1c", [P, 1])
    b2r = ph.sb("b2r", [1, D])
    g_row = ph.sb("g_row", [P, D])
    beta_row = ph.sb("beta_row", [P, D])
    inT = [ph.sb(f"inT{i}", [P, 2, P]) for i in range(2)]
    hid = [ph.sb(f"hid{i}", [P, P]) for i in range(2)]
    n = ph.sb("n", [P, NW, D])
    p_in = [ph.ps(f"p_in{i}", [P, 512]) for i in range(2)]
    last = layer == 1
    s_w, s_T, s_inT, s_z, s_hid, s_m, s_s, s_ch, s_h = (ph.sem(v) for v in (
        "weights", "T", "inT", "z", "hidden", "m", "s", "chain", "h"))
    ln_v, ln_s, ln_g, s_ln = node_norm(nc, ph, K.sum, n, relu=False)
    if not last:
        np_t, np_s, np_v, np_sp = node_products(
            nc, ph, K, K.h, s_h, 1, wn, 2 * D,
            lambda t, row, row3: [(dr.near[t * P:(t + 1) * P, :], row3[:, :, :].rearrange("p i d -> p (i d)")),
                              (dr.far[t * P:(t + 1) * P, :], row[:, D:2 * D])], parts=True)
    p_z = [ph.ps(f"p_z{i}", [P, 512]) for i in range(1)] * 2
    p_m = [ph.ps(f"p_m{i}", [P, 512]) for i in range(1)] * 2

    with ph.block() as block:
        @block.sync
        def _(sp):
            sp.dma_start(w1[:, 0, :], W1[0:D, :]).then_inc(s_w, 16)
            sp.dma_start(w1[:, 1, :], W1[D:2 * D, :]).then_inc(s_w, 16)
            sp.dma_start(w2[:, :], W2).then_inc(s_w, 16)
            column(sp, b1c[:, :], b1, s_w)
            sp.dma_start(b2r[:, :], b2.rearrange("(a d) -> a d", a=1)).then_inc(s_w, 16)
            broadcast_row(sp, g_row[:, :], g, s_w)
            broadcast_row(sp, beta_row[:, :], beta, s_w)
            for i in range(2):
                sp.dma_start(wn[:, i * D:(i + 1) * D], A["L1_gnn_eW1"][1, i * D:(i + 1) * D, :]).then_inc(s_w, 16)
            if not last:
                np_sp(sp)

        @block.gpsimd
        def _(pool):
            ln_g(pool, K)

        @block.tensor
        def _(pe):
            pe.wait_ge(s_w, 144)
            for turn in range(NT + 2):
                t = turn
                if t < NT:
                    if t >= 2:
                        pe.wait_ge(s_inT, t - 1)
                    nc.tensor.transpose(p_in[t % 2][:, 0:P], K.h[:, t, :], K.ident[:, :])
                    nc.tensor.transpose(p_in[t % 2][:, P:2 * P], K.agg[:, t, :], K.ident[:, :]).then_inc(s_T, 1)
                t = turn - 1
                if 0 <= t < NT:
                    pe.wait_ge(s_inT, t + 1)
                    if t >= 1:
                        pe.wait_ge(s_hid, t)
                    for i in range(2):
                        ins = nc.tensor.matmul(p_z[0][:, 0:P], w1[:, i, :], inT[t % 2][:, i, :],
                                               start=(i == 0), stop=(i == 1))
                    ins.then_inc(s_z, 1)
                t = turn - 2
                if 0 <= t < NT:
                    pe.wait_ge(s_hid, t + 1)
                    if t >= 1:
                        pe.wait_ge(s_s, t)
                    nc.tensor.matmul(p_m[0][:, 0:P], K.ones[0:1, :], b2r[:, :], start=True, stop=False)
                    nc.tensor.matmul(p_m[0][:, 0:P], hid[t % 2][:, :], w2[:, :], start=False, stop=True).then_inc(s_m, 1)
            if not last:
                np_t(pe)

        @block.scalar
        def _(act):
            act.wait_ge(s_w, 144)
            for turn in range(NT + 2):
                t = turn
                if t < NT:
                    act.wait_ge(s_T, t + 1)
                    if t >= 2:
                        act.wait_ge(s_z, t - 1)
                    nc.scalar.activation(inT[t % 2][:, :, :].rearrange("p i d -> p (i d)"), p_in[t % 2][:, 0:2 * P],
                                         ACT.Copy).then_inc(s_inT, 1)
                t = turn - 1
                if 0 <= t < NT:
                    act.wait_ge(s_z, t + 1)
                    if t >= 2:
                        act.wait_ge(s_m, t - 1)
                    nc.scalar.activation(hid[t % 2][:, :], p_z[0][:, 0:P], ACT.Silu, bias=b1c[:, 0:1]).then_inc(s_hid, 1)
                t = turn - 2
                if 0 <= t < NT:
                    act.wait_ge(s_m, t + 1)
                    nc.scalar.activation(K.sum[:, t, :], p_m[0][:, 0:P], ACT.Silu).then_inc(s_s, 1)
            ln_s(act)
            if not last:
                np_s(act)

        @block.vector
        def _(dve):
            ch = Chain(dve, s_ch)
            dve.wait_ge(s_s, NT)
            dve.wait_ge(s_w, 144)
            ln_v(dve)
            dve.wait_ge(s_ln, 1)
            wide = lambda v: v[:, :].unsqueeze(1).to_broadcast([P, NW, D])
            ch(nc.vector.tensor_tensor(n[:, :, :], n[:, :, :], wide(g_row), ALU.mult))
            ch(nc.vector.tensor_tensor(n[:, :, :], n[:, :, :], wide(beta_row), ALU.add))
            nc.vector.tensor_tensor(K.h[:, :, :], K.h[:, :, :], n[:, :, :], ALU.add).then_inc(s_h, 1)
            if last:
                dve.wait_ge(s_h, 1)
                nc.vector.tensor_tensor(K.x[:, :, :], K.x[:, :, :], K.h[:, :, :], ALU.add)
            else:
                np_v(dve)
    ph.close()


def gather_pass(nc, K, lay, table, cols):
    ph = Phase(nc, f"gat{lay.key}")
    G = lay.groups
    chunks = 4 // lay.per
    n_tab = max(c for c in cols if c is not None) + 1
    tabs = ph.sb("tabs", [P, n_tab, G * 4])
    tile_row = ph.sb("tile_row", [1, P * lay.per], I32)
    idx = [ph.sb(f"idx{i}", [P, 4], I32) for i in range(2)]
    rows = [ph.sb(f"rows{i}", [P, 4, D]) for i in range(2)]
    hot = [ph.sb(f"hot{i}", [P, 4, P]) for i in range(2)]
    p_s = [ph.ps(f"p_s{i}", [P, 512]) for i in range(2)]
    s_tab, s_idx, s_turn, s_hot, s_sum, s_add = (ph.sem(v) for v in ("tables", "idx", "turn", "hot", "sums", "added"))
    s_rows = [ph.sem(f"rows{i}") for i in range(2)]
    with ph.block() as block:
        @block.sync
        def _(sp):
            sp.dma_start(tabs[:, :, :].rearrange("p i c -> p (i c)"), lay.tabs[:, 0:n_tab * G * 4]).then_inc(s_tab, 16)
            sp.dma_start(tile_row[:, :], lay.tiles).then_inc(s_tab, 16)

        @block.gpsimd
        def _(pool):
            def gather(u):
                if not u.first:
                    pool.wait_ge(s_sum, u.t - 1)
                pool.wait_ge(s_idx, u.t + 1)
                pool.sem_inc(s_turn, 1)
                for k in range(4):
                    pool.indirect_dma_start(out=rows[u.par][:, k, :], out_offset=None, in_=table,
                                            in_offset=bass.IndirectOffsetOnAxis(ap=idx[u.par][:, k:k + 1], axis=0))\
                        .then_inc(s_rows[u.par], 16)
            pipelined(pool, G, None, gather)

        @block.tensor
        def _(pe):
            def sums(u):
                pe.wait_ge(s_hot, u.t + 1)
                pe.wait_ge(s_rows[u.par], (u.use + 1) * 64)
                if not u.first:
                    pe.wait_ge(s_add, (u.t - 1) * lay.per)
                for k in range(4):
                    i = k // chunks
                    ins = nc.tensor.matmul(p_s[u.par][:, i * D:(i + 1) * D], hot[u.par][:, k, :], rows[u.par][:, k, :],
                                           start=(k % chunks == 0), stop=(k % chunks == chunks - 1))
                ins.then_inc(s_sum, 1)
            pipelined(pe, G, None, None, sums)

        @block.vector
        def _(dve):
            nc.vector.memset(K.sum[:, :, :], 0.0)
            dve.wait_ge(s_tab, 32)

            def indices(u):
                if not u.first:
                    dve.wait_ge(s_rows[u.par], u.use * 64)
                nc.vector.tensor_scalar(idx[u.par][:, :], tabs[:, cols[0], bass.ds(u.t * 4, 4)], 0.0, None, ALU.add)\
                    .then_inc(s_idx, 1)

            def places(u):
                if not u.first:
                    dve.wait_ge(s_sum, u.t - 1)
                for k in range(4):
                    at = bass.ds(u.t * 4 + k, 1)
                    if cols[2] is None:
                        ins = nc.vector.tensor_scalar(hot[u.par][:, k, :], K.iota_row[:, 0:P], tabs[:, cols[1], at],
                                                      None, ALU.is_equal)
                    else:
                        ins = nc.vector.tensor_scalar(hot[u.par][:, k, :], K.iota_row[:, 0:P], tabs[:, cols[1], at],
                                                      tabs[:, cols[2], at], ALU.is_equal, ALU.mult)
                ins.then_inc(s_hot, 1)

            def add(u):
                dve.wait_ge(s_sum, u.t + 1)
                for k in range(lay.per):
                    at = dve.value_load(tile_row[0:1, bass.ds(u.t * lay.per + k, 1)], min_val=0, max_val=(NT - 1) * P)
                    if k > 0 or not (isinstance(u.t, int) and u.t == 0):
                        dve.wait_ge(s_add, u.t * lay.per + k)
                    total = K.sum[:, :, :].rearrange("p t d -> p (t d)")[:, bass.ds(at, D)]
                    nc.vector.tensor_tensor(total, p_s[u.par][:, k * D:(k + 1) * D], total, ALU.add).then_inc(s_add, 1)
            pipelined(dve, G, indices, places, None, add, order=(3, 1, 0))
    ph.close()


def conv_input(nc, A, K, dr):
    ph = Phase(nc, "conv")
    w = ph.sb("w", [P, D])
    wT = ph.sb("wT", [P, D])
    b = ph.sb("b", [P, D])
    p_w = ph.ps("p_w", [P, 512])
    s_ld, s_T, s_wT = (ph.sem(v) for v in ("loaded", "T", "wT"))
    ln_v, ln_s, ln_g, s_ln = node_norm(nc, ph, K.x, K.h)
    np_t, np_s, np_v, np_sp = node_products(
        nc, ph, K, K.h, s_ln, 1, wT, D, lambda t, row, row3: [(dr.hidden[t * P:(t + 1) * P, :], row[:, :])], bias=b[:, :])
    with ph.block() as block:
        @block.sync
        def _(sp):
            sp.dma_start(w[:, :], A["L2_gnn_W"]).then_inc(s_ld, 16)
            broadcast_row(sp, b[:, :], A["L2_gnn_b"], s_ld)
            np_sp(sp)

        @block.gpsimd
        def _(pool):
            ln_g(pool, K)

        @block.scalar
        def _(act):
            ln_s(act)
            np_s(act)

        @block.tensor
        def _(pe):
            pe.wait_ge(s_ld, 32)
            nc.tensor.transpose(p_w[:, 0:D], w[:, :], K.ident[:, :]).then_inc(s_T, 1)
            pe.wait_ge(s_wT, 1)
            np_t(pe)

        @block.vector
        def _(dve):
            dve.wait_ge(s_ld, 32)
            dve.wait_ge(s_T, 1)
            nc.vector.tensor_copy(wT[:, :], p_w[:, 0:D]).then_inc(s_wT, 1)
            ln_v(dve)
            np_v(dve)
    ph.close()


def typed_input(nc, A, K, dr):
    ph = Phase(nc, "typed")
    T = 8
    w = ph.sb("w", [P, (T + 1) * D])
    s_ld, s_x = ph.sem("loaded"), ph.sem("x")
    ln_v, ln_s, ln_g, s_ln = node_norm(nc, ph, K.x, K.h)
    np_t, np_s, np_v, np_sp = node_products(
        nc, ph, K, K.h, s_ln, 1, w, (T + 1) * D,
        lambda t, row, row3: [(dr.typed[t * P:(t + 1) * P, :], row[:, 0:T * D]), (dr.o[:, t * D:(t + 1) * D], row[:, T * D:])])
    with ph.block() as block:
        @block.sync
        def _(sp):
            for t in range(T):
                sp.dma_start(w[:, t * D:(t + 1) * D], A["L3_gnn_W_w"][t]).then_inc(s_ld, 16)
            sp.dma_start(w[:, T * D:], A["L3_gnn_W_res"]).then_inc(s_ld, 16)
            np_sp(sp)

        @block.gpsimd
        def _(pool):
            ln_g(pool, K)

        @block.scalar
        def _(act):
            ln_s(act)
            np_s(act)

        @block.tensor
        def _(pe):
            pe.wait_ge(s_ld, (T + 1) * 16)
            np_t(pe)

        @block.vector
        def _(dve):
            nc.vector.tensor_tensor(K.x[:, :, :], K.x[:, :, :], K.sum[:, :, :], ALU.add).then_inc(s_x, 1)
            dve.wait_ge(s_x, 1)
            ln_v(dve)
            np_v(dve)
    ph.close()


def finish(nc, A, K, dr, out):
    ph = Phase(nc, "fin")
    o = ph.sb("o", [P, NW, D])
    e = ph.sb("e", [P, NW, D])
    b = ph.sb("b", [P, D])
    s_ld, s_m, s_e, s_ch, s_x, s_out, s_z = (ph.sem(v) for v in ("loaded", "clipped", "exp", "chain", "x", "out", "zeroed"))
    with ph.block() as block:
        @block.sync
        def _(sp):
            sp.dma_start(o[:, 0:NT, :].rearrange("p t d -> p (t d)"), dr.o[:, :]).then_inc(s_ld, 16)
            broadcast_row(sp, b[:, :], A["L3_gnn_b_res"], s_ld)
            sp.wait_ge(s_x, 1)
            sp.dma_start(out[0:(NT - 1) * P, :].rearrange("(t p) d -> p t d", p=P), K.x[:, 0:NT - 1, :]).then_inc(s_out, 16)
            sp.dma_start(out[(NT - 1) * P:N, :], K.x[0:NLAST, NT - 1, :]).then_inc(s_out, 16)
            sp.wait_ge(s_out, 32)

        @block.scalar
        def _(act):
            act.wait_ge(s_m, 1)
            nc.scalar.activation(e[:, 0:NT, :], e[:, 0:NT, :], ACT.Exp).then_inc(s_e, 1)

        @block.vector
        def _(dve):
            ch = Chain(dve, s_ch)
            v = lambda a: a[:, 0:NT, :]
            dve.wait_ge(s_ld, 32)
            ch(nc.vector.tensor_tensor(v(o), v(o), b[:, :].unsqueeze(1).to_broadcast([P, NT, D]), ALU.add))
            ch(nc.vector.tensor_tensor(v(o), v(o), v(K.sum), ALU.add))
            nc.vector.tensor_scalar(v(e), v(o), 0.0, None, ALU.min).then_inc(s_m, 1)
            ch(nc.vector.tensor_scalar(v(o), v(o), 0.0, 1.0, ALU.max, ALU.subtract))
            ch(nc.vector.tensor_tensor(v(K.x), v(K.x), v(o), ALU.add))
            dve.wait_ge(s_e, 1)
            nc.vector.tensor_tensor(v(K.x), v(K.x), v(e), ALU.add).then_inc(s_x, 1)
    ph.close()


class Names:
    pass


def gnn_program(nc, A, out):
    K, dr = Names(), Names()

    def dram(name, shape, dt=F32):
        return nc.dram_tensor(name, shape, dt).ap()
    dr.attT = dram("attr_T", (3, SLOTS))
    dr.dlrow = dram("dst_row", (1, SLOTS), BF16)
    dr.x0, dr.x0share, dr.x0w, dr.o = (dram(name + "_nodes", (P, NT * D)) for name in ("x0", "x0share", "x0w", "o"))
    dr.ea = [dram(f"edge_features{i}", (P, SLOTS)) for i in range(2)]
    dr.far, dr.hidden = (dram(name + "_rows", (NT * P, D)) for name in ("far", "hidden"))
    dr.near = dram("near_rows", (NT * P, 3 * D), BF16)
    dr.typed = dram("typed_rows", (NT * P, 8 * D))
    ctx = ExitStack()
    with ctx:
        def sb(name, shape, dt=F32):
            return ctx.enter_context(nc.sbuf_tensor(name, shape, dt))
        K.iota_row = sb("iota_row", [P, GS])
        K.iota_p = sb("iota_p", [P, 1])
        K.ident = sb("ident", [P, P])
        K.ones = sb("ones", [P, P])
        K.ones_bf = sb("ones_bf", [P, P], BF16)
        K.neghalf = sb("neghalf", [P, NW])
        dr.by_src, dr.by_dst, dr.units = Names(), Names(), Names()
        for lay, name, key, unit, groups, n_tab in ((dr.by_src, "by_src", 0, US, GU, 3), (dr.by_dst, "by_dst", 1, GS, G, 6),
                                                    (dr.units, "dst_units", 1, US, GU, 2)):
            lay.name, lay.key, lay.fields = name, key, REC if key else REC2
            lay.unit, lay.per, lay.groups, lay.n_tab = unit, GS // unit, groups, n_tab
            lay.rec = dr.by_dst.rec if lay is dr.units else dram(name + "_records", (REC_ROWS, lay.fields))
            lay.tabs = dram(name + "_tables", (P, n_tab * groups * 4))
            if not key:
                lay.unsorted = dram(name + "_unsorted", (EP, EC * REC2))
                lay.rank = dram(name + "_ranks", (EP, EC), I32)
            lay.grp = sb(name + "_grp", [P, 3, lay.per])
            lay.off_i = sb(name + "_off", [P, lay.per], I32)
            lay.tiles = dram(name + "_unit_tiles", (1, P * lay.per), I32)
        dr.by_dst.tile_row = sb("by_dst_tile_row", [1, P], I32)
        K.deg = sb("deg", [P, 2, NW])
        K.norm = sb("norm", [P, 2, NW])
        K.norm8 = sb("norm8", [P, NW])
        K.scr = sb("scr", [P, 2])
        K.eps = sb("eps", [P, 2])
        K.w12 = sb("w12", [P, D])
        K.b12 = sb("b12", [1, D])
        constants(nc, K)
        edge_layout(nc, A, K, dr.by_dst, (dr.by_dst, dr.units))
        edge_tables(nc, K, dr, dr.by_dst)
        edge_tables(nc, K, dr, dr.units)
        start_nodes(nc, A, K, dr)
        fuse_weights(nc, A, K, dr)
        edge_layout(nc, A, K, dr.by_src, (dr.by_src,))
        with nc.sbuf_tensor("adj", [P, NT, NT * P], BF16) as adj:
            K.adj = adj
            adjacency(nc, K, dr)
            hops(nc, K, dr)
        edge_tables(nc, K, dr, dr.by_src)
        K.x, K.h, K.sum, K.agg = (sb("nodes_" + name, [P, NW, D]) for name in ("x", "h", "sum", "agg"))
        gnn_input(nc, A, K, dr)
        edge_pass(nc, A, K, dr, EMBED)
        edge_pass(nc, A, K, dr, LAYER0)
        node_update(nc, A, K, dr, 0)
        edge_pass(nc, A, K, dr, LAYER1)
        node_update(nc, A, K, dr, 1)
        conv_input(nc, A, K, dr)
        gather_pass(nc, K, dr.by_src, dr.hidden[:, :], (0, 1, 2))
        typed_input(nc, A, K, dr)
        gather_pass(nc, K, dr.units, dr.typed.rearrange("n (t d) -> (n t) d", d=D), (0, 1, None))
        finish(nc, A, K, dr, out)


_INS = ["x", "src", "dst", "edge_attr_3", "edge_type_8", "edge_weight",
        "L0_gnn_W1", "L0_gnn_b1", "L0_gnn_W2", "L0_gnn_b2", "L0_gnn_eps1", "L0_gnn_eps2",
        "L1_gnn_emb_W1", "L1_gnn_emb_b1", "L1_gnn_emb_W2", "L1_gnn_emb_b2", "L1_gnn_emb_g", "L1_gnn_emb_beta",
        "L1_gnn_eW1", "L1_gnn_eb1", "L1_gnn_eW2", "L1_gnn_eb2", "L1_gnn_eg", "L1_gnn_ebeta",
        "L1_gnn_nW1", "L1_gnn_nb1", "L1_gnn_nW2", "L1_gnn_nb2", "L1_gnn_ng", "L1_gnn_nbeta",
        "L2_gnn_W", "L2_gnn_b", "L3_gnn_W_w", "L3_gnn_W_res", "L3_gnn_b_res"]


def kernel(**inputs):
    import numpy as np
    import concourse.bacc as bacc
    from concourse.bass_utils import run_bass_kernel_spmd

    nc = bacc.Bacc("TRN2", target_bir_lowering=False, num_devices=1)
    arrays, A = {}, {}
    for name in _INS:
        a = np.ascontiguousarray(inputs[name])
        arrays[f"in_{name}"] = a
        A[name] = nc.dram_tensor(f"in_{name}", a.shape, mybir.dt.from_np(a.dtype), kind="ExternalInput").ap()
    out = nc.dram_tensor("out_x", (N, D), F32, kind="ExternalOutput").ap()
    gnn_program(nc, A, out)
    r = run_bass_kernel_spmd(nc, [arrays], core_ids=[0])
    return r.results[0]["out_x"]
```
